# Optimizing a Trainium2 kernel written in Bass

```python
import numpy as np
import jax
import jax.numpy as jnp

def _softmax(x, axis=-1):
    return jax.nn.softmax(x, axis=axis)

def _gelu(x):
    return jax.nn.gelu(x, approximate=True)

def _silu(x):
    return jax.nn.silu(x)

def _sigmoid(x):
    return jax.nn.sigmoid(x)

def _layernorm(x, axis=-1, eps=1e-05):
    m = jnp.mean(x, axis=axis, keepdims=True)
    v = jnp.var(x, axis=axis, keepdims=True)
    return (x - m) / jnp.sqrt(v + eps)

def _scatter_add(tgt, idx, src, axis=0):
    return tgt.at[idx].add(src)

def _segment_sum(src, seg, n):
    return jax.ops.segment_sum(src, seg, n)
kernel_name = 'mk_prb_d1_jaxref_r4_b4c94a'

def setup_inputs(seed: int=0):
    np.random.seed(seed)
    _w = jnp.asarray

    def _L0_attn_setup():
        import jax, jax.numpy as jnp
        import numpy as np
        EMB = 256
        HEADS = 16
        HEAD_DIM = EMB // HEADS
        MAX_LEN = 250
        key = jax.random.key(seed)
        ks = jax.random.split(key, 11)
        s = 0.02
        x = jax.random.normal(ks[0], (4, 256, EMB), dtype=jnp.float32)
        Wq = jax.random.normal(ks[1], (EMB, EMB), dtype=jnp.float32) * s
        bq = jnp.zeros((EMB,), dtype=jnp.float32)
        Wk = jax.random.normal(ks[2], (EMB, EMB), dtype=jnp.float32) * s
        bk = jnp.zeros((EMB,), dtype=jnp.float32)
        Wv = jax.random.normal(ks[3], (EMB, EMB), dtype=jnp.float32) * s
        bv = jnp.zeros((EMB,), dtype=jnp.float32)
        Wp = jax.random.normal(ks[4], (EMB, EMB), dtype=jnp.float32) * s
        bp = jnp.zeros((EMB,), dtype=jnp.float32)
        bias_table = jax.random.normal(ks[5], (2 * MAX_LEN - 1, HEADS), dtype=jnp.float32) * 0.02
        temperature = jnp.ones((1,), dtype=jnp.float32)
        return {'x': x, 'Wq': Wq, 'bq': bq, 'Wk': Wk, 'bk': bk, 'Wv': Wv, 'bv': bv, 'Wp': Wp, 'bp': bp, 'bias_table': bias_table, 'temperature': temperature}
    _L0_attn_in = _L0_attn_setup()

    def _L0_ffn_setup():
        import jax, jax.numpy as jnp
        import numpy as np

        def _binarize(w):
            alpha = jax.lax.stop_gradient(jnp.mean(jnp.abs(w), axis=1, keepdims=True))
            bw = alpha * jnp.sign(w)
            return w + jax.lax.stop_gradient(bw - w)
        key = jax.random.key(seed)
        k1, k2, k3, k4, k5 = jax.random.split(key, 5)
        D, H = (256, 1024)
        x = jax.random.normal(k1, (64, 196, D), dtype=jnp.float32)
        w1 = jax.random.normal(k2, (H, D), dtype=jnp.float32) * 0.02
        b1 = jax.random.normal(k3, (H,), dtype=jnp.float32) * 0.02
        w2 = jax.random.normal(k4, (D, H), dtype=jnp.float32) * 0.02
        b2 = jax.random.normal(k5, (D,), dtype=jnp.float32) * 0.02
        return {'x': x, 'w1': w1, 'b1': b1, 'w2': w2, 'b2': b2}
    _L0_ffn_in = _L0_ffn_setup()
    _d = {'L0_attn_x': _L0_attn_in['x'], 'L0_attn_Wq': _L0_attn_in['Wq'], 'L0_attn_bq': _L0_attn_in['bq'], 'L0_attn_Wk': _L0_attn_in['Wk'], 'L0_attn_bk': _L0_attn_in['bk'], 'L0_attn_Wv': _L0_attn_in['Wv'], 'L0_attn_bv': _L0_attn_in['bv'], 'L0_attn_Wp': _L0_attn_in['Wp'], 'L0_attn_bp': _L0_attn_in['bp'], 'L0_attn_bias_table': _L0_attn_in['bias_table'], 'L0_attn_temperature': _L0_attn_in['temperature'], 'L0_ffn_w1': _L0_ffn_in['w1'], 'L0_ffn_b1': _L0_ffn_in['b1'], 'L0_ffn_w2': _L0_ffn_in['w2'], 'L0_ffn_b2': _L0_ffn_in['b2']}
    _x0 = _d['L0_attn_x']
    _d['L0_attn_x'] = jax.random.normal(jax.random.fold_in(jax.random.key(seed), 1), (4, 2048, 256), dtype=_x0.dtype)
    del _x0
    return _d

def reference(L0_attn_x, L0_attn_Wq, L0_attn_bq, L0_attn_Wk, L0_attn_bk, L0_attn_Wv, L0_attn_bv, L0_attn_Wp, L0_attn_bp, L0_attn_bias_table, L0_attn_temperature, L0_ffn_w1, L0_ffn_b1, L0_ffn_w2, L0_ffn_b2):

    def _L0_attn_ref(x, Wq, bq, Wk, bk, Wv, bv, Wp, bp, bias_table, temperature):
        import jax, jax.numpy as jnp
        import numpy as np
        EMB = 256
        HEADS = 16
        HEAD_DIM = EMB // HEADS
        MAX_LEN = 250
        B, N, C = x.shape
        H, D = (HEADS, C // HEADS)

        def split_heads(t):
            return t.reshape(B, N, H, D).transpose(0, 2, 1, 3)
        q = split_heads(x @ Wq + bq)
        k = split_heads(x @ Wk + bk)
        v = split_heads(x @ Wv + bv)
        energy = jnp.einsum('bhqd,bhkd->bhqk', q, k)
        pos = jnp.arange(N)
        rel = pos[:, None] - pos[None, :] + (N - 1)
        rel = jnp.clip(rel, 0, bias_table.shape[0] - 1)
        bias = bias_table[rel].transpose(2, 0, 1)
        energy = energy + bias[None]
        scaling = jnp.sqrt(jnp.float32(C))
        temp = jnp.clip(temperature[0], 0.1, 10.0)
        att = jax.nn.softmax(energy / (scaling * temp), axis=-1)
        out = jnp.einsum('bhqk,bhkd->bhqd', att, v)
        out = out.transpose(0, 2, 1, 3).reshape(B, N, C)
        return out @ Wp + bp

    def _L0_ffn_ref(x, w1, b1, w2, b2):
        import jax, jax.numpy as jnp
        import numpy as np

        def _binarize(w):
            alpha = jax.lax.stop_gradient(jnp.mean(jnp.abs(w), axis=1, keepdims=True))
            bw = alpha * jnp.sign(w)
            return w + jax.lax.stop_gradient(bw - w)
        bw1 = _binarize(w1)
        h = jnp.einsum('bsd,hd->bsh', x, bw1) + b1
        h = jax.nn.gelu(h, approximate=False)
        bw2 = _binarize(w2)
        out = jnp.einsum('bsh,dh->bsd', h, bw2) + b2
        return out
    x = L0_attn_x
    xn = _layernorm(x, axis=-1)
    x = x + _L0_attn_ref(xn, L0_attn_Wq, L0_attn_bq, L0_attn_Wk, L0_attn_bk, L0_attn_Wv, L0_attn_bv, L0_attn_Wp, L0_attn_bp, L0_attn_bias_table, L0_attn_temperature) + _L0_ffn_ref(xn, L0_ffn_w1, L0_ffn_b1, L0_ffn_w2, L0_ffn_b2)
    return x

_drawn_inputs = setup_inputs


def setup_inputs(seed=0):
    import zlib

    import numpy as np

    out = dict(_drawn_inputs(seed))
    spreads = {'L0_attn_bq': (0.0, 0.8),
     'L0_attn_bk': (0.0, 0.8),
     'L0_attn_bv': (0.0, 0.1),
     'L0_attn_bp': (0.0, 0.1)}
    factors = {'L0_attn_Wq': 8.0,
     'L0_attn_Wk': 8.0,
     'L0_attn_Wv': 8.0,
     'L0_attn_bias_table': 8.0,
     'L0_ffn_b1': 8.0,
     'L0_ffn_b2': 2.933}
    for name, (base, spread) in spreads.items():
        noise = np.random.default_rng([zlib.crc32(name.encode()), seed]).standard_normal(out[name].shape)
        drawn = base * np.exp(spread * noise) if base else spread * noise
        out[name] = jnp.asarray(drawn.astype(out[name].dtype))
    for name, factor in factors.items():
        out[name] = (out[name] * factor).astype(out[name].dtype)
    return out
```

```python
from contextlib import ExitStack

import concourse.bass as bass
from concourse import mybir

ALU = mybir.AluOpType
ACT = mybir.ActivationFunctionType
AX = mybir.AxisListType
F32 = mybir.dt.float32
BF16 = mybir.dt.bfloat16

P = 128
BATCH, TOKENS, EMB = 4, 2048, 256
HEADS = 16
HDIM = EMB // HEADS
HIDDEN = 1024
TABLE = 499
EPS = 1e-5

KT = EMB // P
HT = HIDDEN // P
CHUNK = 512
TPC = CHUNK // P
CHUNKS = BATCH * TOKENS // CHUNK
CPB = TOKENS // CHUNK
NHEAD = BATCH * HEADS
QT = TOKENS // P
PARTS = 3
PAIRS = 6
SROWS = PAIRS * HDIM
MROWS = SROWS + PARTS
SLOTS = 3
VCOLS = 32
STEPS = QT
UNITS = 4
AHEAD = 4
FIRST_KEY = TOKENS - CHUNK
ORDER = "0u1uvuu"
WWIDE = CHUNK + 3 * P
REV = CHUNK + P - 2
DELTA = 1024
ITEMS = 2 * KT


TURN_BANKS = (4, 5, 7)
ALL_UNITS = QT * UNITS
ATT_AT = UNITS
PEAK_AT = UNITS * (STEPS - AHEAD + 1)
EARLY = ALL_UNITS + AHEAD * UNITS
EARLY_PEAK_AT = ALL_UNITS + UNITS


def place_of(unit, early=False):
    if early:
        return unit + (unit >= EARLY_PEAK_AT)
    return unit + (unit >= ATT_AT) + (unit >= PEAK_AT)


ATT_PLACE, PEAK_PLACE, EARLY_PEAK_PLACE = ATT_AT, PEAK_AT + 1, EARLY_PEAK_AT
PLACES = place_of(ALL_UNITS)
UNIT_AT = {place_of(u): u for u in range(ALL_UNITS)}


def bank_at(place):
    return TURN_BANKS[place % 3]


def at_least(engine, sem, value):
    if isinstance(value, int) and value <= 0:
        return
    engine.wait_ge(sem, value)


def build(nc, x, wq, bq, wk, bk, wv, bv, wp, bp, table, temperature, w1, b1, w2, b2, out):
    with ExitStack() as ctx:
        def sb(name, shape, dt=F32):
            return ctx.enter_context(nc.sbuf_tensor(name, shape, dt))

        def sem(name):
            return ctx.enter_context(nc.semaphore(name))

        parts_dram = nc.dram_tensor("parts_dram", [2, PARTS, BATCH * EMB, TOKENS], BF16).ap()
        base_dram = nc.dram_tensor("base_dram", [BATCH * TOKENS, EMB], F32).ap()
        delta_dram = nc.dram_tensor("delta_dram", [2, HEADS, DELTA], F32).ap()

        ident = sb("ident", [P, P])
        ident16 = sb("ident16", [P, P], BF16)
        scale = sb("scale", [P, 1])
        wproj = sb("wproj", [P, KT, EMB])
        vo = sb("vo", [P, NHEAD, QT, HDIM])

        wq_sb = sb("wq_sb", [P, KT, EMB])
        wk_sb = sb("wk_sb", [P, KT, EMB])
        wv_sb = sb("wv_sb", [P, KT, EMB])
        sign1 = sb("sign1", [P, KT, HIDDEN], BF16)
        sign2 = sb("sign2", [P, HT, EMB])
        alpha1 = sb("alpha1", [P, HT])
        alpha2 = sb("alpha2", [P, KT])
        alpha2_row = sb("alpha2_row", [P, EMB])
        bq_col = sb("bq_col", [P, KT])
        bk_col = sb("bk_col", [P, KT])
        b1_col = sb("b1_col", [P, HT])
        bv_row = sb("bv_row", [P, EMB])
        b2_row = sb("b2_row", [P, EMB])
        bp_row = sb("bp_row", [P, EMB])
        x_in = sb("x_in", [P, 2, TPC, EMB])
        stats = sb("stats", [P, TPC, 6])
        wait_here = sb("wait_here", [P, 1])
        moments = sb("moments", [P, TPC, 2])
        std = sb("std", [P, TPC])
        rstd = sb("rstd", [P, TPC])
        eps_col = sb("eps_col", [P, 1])
        xn = sb("xn", [P, TPC, EMB])
        xt = sb("xt", [P, KT, CHUNK])
        xt_rest = sb("xt_rest", [P, KT, CHUNK])
        xt_parts = sb("xt_parts", [P, PARTS, KT, CHUNK], BF16)
        hid = sb("hid", [P, HT, CHUNK])
        qk_val = sb("qk_val", [P, 2, CHUNK])
        qk_rest = sb("qk_rest", [P, 2, CHUNK])
        qk_part = sb("qk_part", [P, 2, PARTS, CHUNK], BF16)
        base = sb("base", [P, TPC, EMB])

        stack_room = sb("stack_room", [P, 2, SLOTS, TOKENS], BF16)
        q_stack = stack_room[:, 0]
        k_stack = stack_room[:, 1]
        exps = sb("exps", [P, 2, TOKENS])
        v_ones = sb("v_ones", [P, QT, VCOLS])
        bias_max = sb("bias_max", [P, WWIDE])
        bias_exp = sb("bias_exp", [P, CHUNK])
        peaks = sb("peaks", [P, QT, UNITS])
        peak = sb("peak", [P, QT])
        zeros = sb("zeros", [P, QT])
        neg_peak = sb("neg_peak", [P, 2, QT])
        peak_parts = sb("peak_parts", [P, P // QT, QT], BF16)
        peak_rows = sb("peak_rows", [PARTS * QT, P], BF16)
        att_t = sb("att_t", [P, CHUNK])
        rden = sb("rden", [P, TPC, CPB])

        w1_raw = exps[:, 0].rearrange("p (t c) -> p t c", t=HT)
        w2_raw = exps[:, 1].rearrange("p (t c) -> p t c", t=KT)
        sgn_pos = hid[:, 0:4].rearrange("p a b -> p (a b)")
        sgn_neg = hid[:, 4:8].rearrange("p a b -> p (a b)")
        table_in = qk_val[:, 0, 0:4 * HEADS].rearrange("p (t h) -> p t h", t=4)
        table_t = xn[0:HEADS].rearrange("p a b -> p (a b)")
        delta = xt_rest[0:HEADS].rearrange("p a b -> p (a b)")
        delta_rev = qk_rest[0:HEADS].rearrange("p a b -> p (a b)")
        diag = base[:, 0:KT, 0:P]
        all_ones = base[:, KT, 0:P]
        o_in = xn
        o_t = xt
        base_in = x_in

        ps = ctx.enter_context(nc.psum_tensor("ps", [P, 8, CHUNK], F32))

        w_loaded = sem("w_loaded")
        consts = sem("consts")
        ident_ok = sem("ident_ok")
        setup_step = sem("setup_step")
        signs_ok = sem("signs_ok")
        alpha2_turned = sem("alpha2_turned")
        sign_turned = sem("sign_turned")
        sign_copied = sem("sign_copied")
        table_turned = sem("table_turned")
        delta_ok = sem("delta_ok")
        delta_stored = sem("delta_stored")
        x_loaded = sem("x_loaded")
        ln_step = sem("ln_step")
        var_ok = sem("var_ok")
        std_ok = sem("std_ok")
        xn_ok = sem("xn_ok")
        xt_turned = sem("xt_turned")
        xt_ok = sem("xt_ok")
        xt_step = sem("xt_step")
        xt_parts_ok = sem("xt_parts_ok")
        qkv_ready = sem("qkv_ready")
        qkv_taken = sem("qkv_taken")
        h_ready = sem("h_ready")
        h_taken = sem("h_taken")
        y_ready = sem("y_ready")
        y_taken = [sem("y_taken0"), sem("y_taken1")]
        split_step = sem("split_step")
        split_ok = sem("split_ok")
        base_step = sem("base_step")
        base_ok = sem("base_ok")
        base_stored = sem("base_stored")
        part_stored = [sem("part_stored0"), sem("part_stored1")]
        stack_loaded = sem("stack_loaded")
        bias_max_loaded = sem("bias_max_loaded")
        bias_exp_loaded = sem("bias_exp_loaded")
        ones_ok = sem("ones_ok")
        unit_ready = sem("unit_ready")
        unit_done = sem("unit_done")
        peak_ok = sem("peak_ok")
        peak_step = sem("peak_step")
        peak_split = sem("peak_split")
        peak_turned = sem("peak_turned")
        peak_copied = sem("peak_copied")
        peak_loaded = sem("peak_loaded")
        scores_ready = [sem("scores_ready0"), sem("scores_ready1")]
        scores_biased = sem("scores_biased")
        exp_done = [sem("exp_done0"), sem("exp_done1")]
        v_copied = sem("v_copied")
        pv_done = sem("pv_done")
        att_copied = sem("att_copied")
        att_turned = sem("att_turned")
        rden_ok = sem("rden_ok")
        att_ok = sem("att_ok")
        base_loaded = [sem("base_loaded0"), sem("base_loaded1")]
        o_copied = sem("o_copied")
        o_turned = sem("o_turned")
        ot_ok = [sem("ot_ok0"), sem("ot_ok1")]
        proj_ready = sem("proj_ready")
        out_ok = sem("out_ok")
        out_stored = [sem("out_stored0"), sem("out_stored1")]

        x_rows = x.rearrange("b (g t p) c -> p (b g) t c", t=TPC, p=P)
        out_rows = out.rearrange("b (g t p) c -> p (b g) t c", t=TPC, p=P)
        base_rows = base_dram.rearrange("(g t p) c -> p g t c", t=TPC, p=P)

        LOADS = 15
        TURNS = 2 * HT * KT

        block = ctx.enter_context(nc.Block())

        @block.sync
        def _(sp):
            def row(v):
                return bass.AP(tensor=v.tensor, offset=v.offset, ap=[[0, P], [1, v.shape[0]]])

            def weight(w):
                return w.rearrange("(t p) c -> p t c", p=P)

            sp.dma_start(x_in[:, 0], x_rows[:, 0]).then_inc(x_loaded, 16)
            sp.dma_start(w1_raw, w1.rearrange("(t p) c -> p t c", p=P)).then_inc(w_loaded, 16)
            sp.dma_start(w2_raw, w2.rearrange("(t p) c -> p t c", p=P)).then_inc(w_loaded, 16)
            sp.dma_start(table_in[:, 0:3], table[0:3 * P, :].rearrange("(t p) h -> p t h", p=P)).then_inc(w_loaded, 16)
            sp.dma_start(table_in[0:TABLE - 3 * P, 3], table[3 * P:TABLE, :]).then_inc(w_loaded, 16)
            sp.dma_start(scale[:, :], row(temperature)).then_inc(w_loaded, 16)
            sp.dma_start(b1_col[:, :], b1.rearrange("(t p) -> p t", p=P),
                         allow_slow_non_contiguous=True).then_inc(w_loaded, 16)
            sp.dma_start(bq_col[:, :], bq.rearrange("(t p) -> p t", p=P),
                         allow_slow_non_contiguous=True).then_inc(w_loaded, 16)
            sp.dma_start(bk_col[:, :], bk.rearrange("(t p) -> p t", p=P),
                         allow_slow_non_contiguous=True).then_inc(w_loaded, 16)
            sp.dma_start(bv_row[:, :], row(bv)).then_inc(w_loaded, 16)
            sp.dma_start(b2_row[:, :], row(b2)).then_inc(w_loaded, 16)
            sp.dma_start(bp_row[:, :], row(bp)).then_inc(w_loaded, 16)
            sp.dma_start(wq_sb[:], weight(wq)).then_inc(w_loaded, 16)
            sp.dma_start(wk_sb[:], weight(wk)).then_inc(w_loaded, 16)
            sp.dma_start(wv_sb[:], weight(wv)).then_inc(w_loaded, 16)
            sp.dma_start(wproj[:], weight(wp)).then_inc(w_loaded, 16)
            sp.wait_ge(delta_ok, 1)
            sp.dma_start(delta_dram[0], delta).then_inc(delta_stored, 16)
            sp.dma_start(delta_dram[1], delta_rev).then_inc(delta_stored, 16)
            sp.wait_ge(delta_stored, 32)

            def load_x(c):
                sp.dma_start(x_in[:, bass.ds(c % 2, 1)], x_rows[:, bass.ds(c, 1)]).then_inc(x_loaded, 16)

            def store_parts(c):
                rows = (c // CPB) * EMB
                cols = (c % CPB) * CHUNK
                for i in range(ITEMS):
                    sp.wait_ge(split_ok, ITEMS * c + i + 1)
                    dst = parts_dram[i // KT, :, bass.ds(rows + (i % KT) * P, P), bass.ds(cols, CHUNK)]
                    sp.dma_start(dst.rearrange("a r c -> r a c"), qk_part[:, i % 2]).then_inc(part_stored[i % 2], 16)

            def store_base(c):
                sp.wait_ge(base_ok, c + 1)
                sp.dma_start(base_rows[:, bass.ds(c, 1)], base[:]).then_inc(base_stored, 16)

            load_x(1)
            store_parts(0)
            with sp.Fori(1, CHUNKS - 1) as c:
                store_base(c - 1)
                load_x(c + 1)
                store_parts(c)
            store_base(CHUNKS - 2)
            store_parts(CHUNKS - 1)
            store_base(CHUNKS - 1)
            for i in range(2):
                sp.wait_ge(part_stored[i], 16 * 2 * CHUNKS)
            sp.wait_ge(base_stored, 16 * CHUNKS)

            def load_stack(n):
                slot = n % SLOTS
                at_least(sp, stack_loaded, 16 * 12 * n)
                at = 0
                for a in range(PARTS):
                    k = PARTS - a
                    for j in range(k):
                        sp.dma_start(q_stack[at + j * HDIM:at + (j + 1) * HDIM, bass.ds(slot, 1), :],
                                     parts_dram[0, a, bass.ds(n * HDIM, HDIM), :]).then_inc(stack_loaded, 16)
                    for j in range(k):
                        sp.dma_start(k_stack[at + j * HDIM:at + (j + 1) * HDIM, bass.ds(slot, 1), :],
                                     parts_dram[1, j, bass.ds(n * HDIM, HDIM), :]).then_inc(stack_loaded, 16)
                    at += k * HDIM

            def toeplitz(which, n, width):
                r = delta_dram[which, bass.ds(n % HEADS, 1), 0:width]
                return bass.AP(tensor=r.tensor, offset=r.offset, ap=[[1, P], [1, width]])

            def load_bias_max(n):
                if not isinstance(n, int) or n > 0:
                    sp.wait_ge(unit_done, 64 * (n - 1) + 16)
                sp.dma_start(bias_max[:, :], toeplitz(0, n, WWIDE)).then_inc(bias_max_loaded, 16)

            def load_bias_exp(n):
                at_least(sp, scores_biased, 4 * n)
                sp.dma_start(bias_exp[:, :], toeplitz(1, n, CHUNK)).then_inc(bias_exp_loaded, 16)

            def load_peak(n):
                sp.wait_ge(peak_copied, n + 1)
                dst = q_stack[SROWS:MROWS, bass.ds(n % SLOTS, 1), :].rearrange("a s (t p) -> a (s t) p", p=P)
                sp.dma_start(dst, peak_rows[:, :]).then_inc(peak_loaded, 16)

            load_stack(0)
            load_bias_max(0)
            load_stack(1)
            load_bias_max(1)
            load_peak(0)

            def head_loads(n, stack=True, peaks_too=True):
                if stack:
                    at_least(sp, scores_ready[1], QT * n)
                    load_stack(n + 2)
                load_bias_exp(n)
                if stack:
                    load_bias_max(n + 2)
                if peaks_too:
                    load_peak(n + 1)

            head_loads(0)
            with sp.Fori(1, NHEAD - 2) as n:
                head_loads(n)
            head_loads(NHEAD - 2, stack=False)
            head_loads(NHEAD - 1, stack=False, peaks_too=False)

            def load_base(g, j):
                sp.dma_start(base_in[:, j], base_rows[:, bass.ds(g, 1)]).then_inc(base_loaded[j], 16)

            def store_out(g, j):
                sp.wait_ge(out_ok, g + 1)
                sp.dma_start(out_rows[:, bass.ds(g, 1)], base_in[:, j]).then_inc(out_stored[j], 16)

            load_base(0, 0)
            load_base(1, 1)
            with sp.Fori(0, CHUNKS // 2 - 1) as r:
                for j in range(2):
                    store_out(2 * r + j, j)
                    sp.wait_ge(out_stored[j], 16 * (r + 1))
                    load_base(2 * r + j + 2, j)
            for j in range(2):
                store_out(CHUNKS - 2 + j, j)
            for j in range(2):
                sp.wait_ge(out_stored[j], 16 * (CHUNKS // 2))

        @block.tensor
        def _(pe):
            pe.wait_ge(ident_ok, 2)
            pe.wait_ge(w_loaded, 16 * LOADS)
            for t in range(4):
                rows = P if t < 3 else TABLE - 3 * P
                last = pe.transpose(ps[0:HEADS, 7, t * P:t * P + rows], table_in[0:rows, t, :], ident[0:rows, 0:rows])
            last.then_inc(table_turned, 1)
            pe.wait_ge(alpha2_turned, 1)
            for k in range(KT):
                last = pe.matmul(ps[:, 6, k * P:(k + 1) * P], all_ones, diag[:, k], start=True, stop=True)
            last.then_inc(alpha2_turned, 1)
            pe.wait_ge(signs_ok, 1)
            for b in range(TURNS):
                if b >= 4:
                    pe.wait_ge(sign_copied, b - 3)
                second, t = divmod(b, TURNS // 2)
                src = sgn_pos if not second else sgn_neg
                pe.transpose(ps[:, b % 4, 0:P], src[:, t * P:(t + 1) * P], ident[:, :]).then_inc(sign_turned, 1)

            def turn_x(c):
                pe.wait_ge(xn_ok, c + 1)
                for k in range(KT):
                    at_least(pe, xt_ok, KT * c - KT + k + 1)
                    for t in range(TPC):
                        last = pe.transpose(ps[:, k, t * P:(t + 1) * P], xn[:, t, k * P:(k + 1) * P], ident[:, :])
                    last.then_inc(xt_turned, 1)

            def qkv(c):
                pe.wait_ge(xt_ok, KT * (c + 1))
                for i in range(ITEMS + 2):
                    if i < 4:
                        at_least(pe, h_taken, HT * c - 4 + (i + 2) % 4 + 1)
                    else:
                        pe.wait_ge(qkv_taken, 6 * c + i - 3)
                    bank = 2 + i % 4
                    if i < ITEMS:
                        w = wq_sb if i < KT else wk_sb
                        for k in range(KT):
                            last = pe.matmul(ps[:, bank, :], w[:, k, (i % KT) * P:(i % KT + 1) * P], xt[:, k, :],
                                             start=(k == 0), stop=(k == KT - 1))
                    else:
                        for t in range(2):
                            tile = 2 * (i - ITEMS) + t
                            for k in range(KT):
                                last = pe.matmul(ps[:, bank, t * EMB:(t + 1) * EMB], xt[:, k, tile * P:(tile + 1) * P],
                                                 wv_sb[:, k, :], start=(k == 0), stop=(k == KT - 1))
                    last.then_inc(qkv_ready, 1)

            def hidden(c):
                pe.wait_ge(xt_parts_ok, KT * (c + 1))
                for m in range(HT):
                    i = ITEMS + 2 + m
                    if m < 4:
                        pe.wait_ge(qkv_taken, 6 * c + i - 3)
                    else:
                        pe.wait_ge(h_taken, HT * c + m - 3)
                    for k in range(KT):
                        for a in range(PARTS):
                            last = pe.matmul(ps[:, 2 + i % 4, :], sign1[:, k, m * P:(m + 1) * P], xt_parts[:, a, k, :],
                                             start=(k == 0 and a == 0), stop=(k == KT - 1 and a == PARTS - 1))
                    last.then_inc(h_ready, 1)

            def ffn_out(c):
                pe.wait_ge(h_taken, HT * (c + 1))
                for j in range(2):
                    at_least(pe, y_taken[j], c)
                    for t in range(2):
                        tile = 2 * j + t
                        for m in range(HT):
                            last = pe.matmul(ps[:, 6 + j, t * EMB:(t + 1) * EMB], hid[:, m, tile * P:(tile + 1) * P],
                                             sign2[:, m, :], start=(m == 0), stop=(m == HT - 1))
                    last.then_inc(y_ready, 1)

            pe.wait_ge(sign_copied, TURNS)
            pe.wait_ge(consts, 1)
            turn_x(0)
            qkv(0)
            hidden(0)
            def chunk(c):
                turn_x(c)
                ffn_out(c - 1)
                qkv(c)
                hidden(c)

            chunk(1)
            with pe.Fori(2, CHUNKS) as c:
                chunk(c)
            ffn_out(CHUNKS - 1)
            for j in range(2):
                pe.wait_ge(y_taken[j], CHUNKS)
            pe.wait_ge(ones_ok, 3)

            def bank_free(n, place):
                before = place - 3
                if before == ATT_PLACE:
                    if isinstance(n, int) and n == 0:
                        before -= 3
                    else:
                        pe.wait_ge(att_ok, n)
                        return
                if before == PEAK_PLACE:
                    pe.wait_ge(peak_copied, n + 2)
                    return
                if before < 0:
                    unit = before
                else:
                    unit = UNIT_AT[before]
                count = EARLY + ALL_UNITS * n + unit + 1
                pe.wait_ge(unit_done, min(count, ALL_UNITS * NHEAD) if isinstance(n, int) else count)

            def early_bank_free(place):
                before = place - 3
                if before == EARLY_PEAK_PLACE:
                    pe.wait_ge(peak_copied, 1)
                else:
                    at_least(pe, unit_done, before + 1 - (before > EARLY_PEAK_PLACE))

            def units(n, s, body=None, first_unit=0):
                if s == 0:
                    pe.wait_ge(stack_loaded, 16 * 12 * (n + 1))
                for u in range(UNITS):
                    early = body is None
                    place = place_of(first_unit + u, early)
                    if early:
                        early_bank_free(place)
                    else:
                        bank_free(body, place)
                    pe.matmul(ps[:, bank_at(place), :], q_stack[0:SROWS, bass.ds(n % SLOTS, 1), s * P:(s + 1) * P],
                              k_stack[0:SROWS, bass.ds(n % SLOTS, 1), u * CHUNK:(u + 1) * CHUNK],
                              start=True, stop=True).then_inc(unit_ready, 1)
                    yield

            def turn_peak(n):
                pe.wait_ge(peak_split, n + 1)
                if isinstance(n, int) and n == 0:
                    early_bank_free(EARLY_PEAK_PLACE)
                    bank = bank_at(EARLY_PEAK_PLACE)
                else:
                    bank_free(n - 1, PEAK_PLACE)
                    bank = bank_at(PEAK_PLACE)
                pe.transpose(ps[:, bank, :].bitcast(BF16)[:, 0:P],
                             peak_parts[:].rearrange("p a t -> p (a t)"), ident16[:, :]).then_inc(peak_turned, 1)

            def scores(n, kt, half):
                if kt == 0 and half == 0:
                    pe.wait_ge(peak_loaded, 16 * (n + 1))
                at_least(pe, exp_done[half], QT * n + kt)
                for j in range(2):
                    at = (2 * half + j) * CHUNK
                    last = pe.matmul(ps[:, 2 * half + j, :], k_stack[0:MROWS, bass.ds(n % SLOTS, 1), kt * P:(kt + 1) * P],
                                     q_stack[0:MROWS, bass.ds(n % SLOTS, 1), at:at + CHUNK], start=True, stop=True)
                last.then_inc(scores_ready[half], 1)

            def times_v(n, kt):
                for half in range(2):
                    pe.wait_ge(exp_done[half], QT * n + kt + 1)
                if kt % 8 == 0:
                    pe.wait_ge(v_copied, 2 * n + kt // 8 + 1)
                if kt == 0:
                    at_least(pe, att_copied, n)
                for c in range(CPB):
                    last = pe.matmul(ps[c * VCOLS:(c + 1) * VCOLS, 6, :], v_ones[:, kt, :],
                                     exps[:, kt % 2, c * CHUNK:(c + 1) * CHUNK], start=(kt == 0), stop=(kt == QT - 1))
                last.then_inc(pv_done, 1)

            def turn_att(n):
                pe.wait_ge(att_copied, n + 1)
                if isinstance(n, int) and n == NHEAD - 1:
                    pe.wait_ge(att_ok, n)
                else:
                    bank_free(n + 1, ATT_PLACE)
                for t in range(TPC):
                    last = pe.transpose(ps[:, bank_at(ATT_PLACE), t * P:(t + 1) * P], att_t[:, t * P:(t + 1) * P], ident[:, :])
                last.then_inc(att_turned, 1)

            def drain(g):
                for _ in g:
                    pass

            def head(n, first=False, ahead2=True, ahead1=True, more=True):
                for kt in range(1, STEPS + 1):
                    nxt, k = (n, kt) if kt < STEPS else (n + 1, 0)
                    if kt <= STEPS - AHEAD:
                        work = units(n + 1, kt + AHEAD - 1, n, UNITS * (kt - 1)) if ahead1 else iter(())
                    else:
                        work = units(n + 2, kt - (STEPS - AHEAD) - 1, n, UNITS * (kt - 1)) if ahead2 else iter(())
                    if kt == 2 and not first:
                        turn_att(n - 1)
                    if kt == STEPS - AHEAD + 2 and ahead1:
                        turn_peak(n + 1)
                    for turn in ORDER:
                        if turn == "u":
                            next(work, None)
                        elif turn == "v":
                            times_v(n, kt - 1)
                        elif kt < STEPS or more:
                            scores(nxt, k, int(turn))

            for s in range(STEPS):
                drain(units(0, s, None, UNITS * s))
            for s in range(AHEAD):
                drain(units(1, s, None, ALL_UNITS + UNITS * s))
                if s == 0:
                    turn_peak(0)
            for half in range(2):
                scores(0, 0, half)
            head(0, first=True)
            with pe.Fori(1, NHEAD - 2) as n:
                head(n)
            head(NHEAD - 2, ahead2=False)
            head(NHEAD - 1, ahead2=False, ahead1=False, more=False)
            turn_att(NHEAD - 1)
            pe.wait_ge(att_ok, NHEAD)

            def turn_o(g):
                pe.wait_ge(o_copied, g + 1)
                for k in range(KT):
                    at_least(pe, ot_ok[k], g)
                    for t in range(TPC):
                        last = pe.transpose(ps[:, k, t * P:(t + 1) * P], o_in[:, t, k * P:(k + 1) * P], ident[:, :])
                    last.then_inc(o_turned, 1)

            def project(g):
                for k in range(KT):
                    pe.wait_ge(ot_ok[k], g + 1)
                for j in range(2):
                    at_least(pe, out_ok, g)
                    for t in range(2):
                        for k in range(KT):
                            tile = 2 * j + t
                            last = pe.matmul(ps[:, 2 + j, t * EMB:(t + 1) * EMB], o_t[:, k, tile * P:(tile + 1) * P],
                                             wproj[:, k, :], start=(k == 0), stop=(k == KT - 1))
                    last.then_inc(proj_ready, 1)

            turn_o(0)
            project(0)
            with pe.Fori(1, CHUNKS) as g:
                turn_o(g)
                project(g)

        @block.scalar
        def _(act):
            def turned_signs(b):
                act.wait_ge(sign_turned, b + 1)
                second, t = divmod(b, TURNS // 2)
                if not second:
                    dst = sign1[:, t % KT, (t // KT) * P:(t // KT + 1) * P]
                else:
                    dst = sign2[:, t % HT, (t // HT) * P:(t // HT + 1) * P]
                act.activation(dst, ps[:, b % 4, 0:P], ACT.Copy).then_inc(sign_copied, 1)

            for b in range(TURNS):
                turned_signs(b)

            def root(c):
                act.wait_ge(var_ok, c + 1)
                act.activation(std[:, :], moments[:, :, 1], ACT.Sqrt, bias=eps_col[:, 0:1]).then_inc(std_ok, 1)

            def take_xt(c):
                at_least(act, qkv_ready, 6 * c)
                at_least(act, xt_parts_ok, KT * c)
                for k in range(KT):
                    act.wait_ge(xt_turned, KT * c + k + 1)
                    act.activation(xt[:, k, :], ps[:, k, :], ACT.Copy).then_inc(xt_ok, 1)

            def gelus(c, more=True):
                at_least(act, y_ready, 2 * c)
                for m in range(HT):
                    act.wait_ge(h_ready, HT * c + m + 1)
                    act.activation(hid[:, m, :], ps[:, 2 + (ITEMS + 2 + m) % 4, :], ACT.Gelu,
                                   bias=b1_col[:, m:m + 1], scale=alpha1[:, m:m + 1]).then_inc(h_taken, 1)
                    if m == 3 and more:
                        root(c + 1)

            act.wait_ge(consts, 1)
            root(0)
            take_xt(0)
            gelus(0)
            with act.Fori(1, CHUNKS - 1) as c:
                take_xt(c)
                gelus(c)
            take_xt(CHUNKS - 1)
            gelus(CHUNKS - 1, more=False)

            def exp(n, kt):
                at_least(act, pv_done, QT * n + kt - 1)
                for half in range(2):
                    act.wait_ge(scores_ready[half], QT * n + kt + 1)
                    if half == 0 and kt >= QT - 4:
                        act.wait_ge(scores_biased, 4 * n + kt - (QT - 4) + 1)
                    act.activation(exps[:, kt % 2, half * 2 * CHUNK:(half + 1) * 2 * CHUNK],
                                   ps[:, 2 * half:2 * half + 2, :].rearrange("p a b -> p (a b)"),
                                   ACT.Exp).then_inc(exp_done[half], 1)

            def take_att(n):
                act.wait_ge(pv_done, QT * (n + 1))
                at_least(act, att_turned, n)
                act.activation(att_t[:, :], ps[:, 6, :], ACT.Copy).then_inc(att_copied, 1)

            def take_peak(n):
                act.wait_ge(peak_turned, n + 1)
                at_least(act, peak_loaded, 16 * n)
                early = isinstance(n, int) and n == 0
                bank = bank_at(EARLY_PEAK_PLACE if early else PEAK_PLACE)
                act.activation(peak_rows[:, :], ps[:, bank, :].bitcast(BF16)[0:PARTS * QT, 0:P],
                               ACT.Copy).then_inc(peak_copied, 1)

            def head(n, first=False, ahead=True, more=True):
                for kt in range(1, STEPS + 1):
                    if kt == 1 and not first:
                        take_att(n - 1)
                    if kt < STEPS:
                        exp(n, kt)
                    elif more:
                        exp(n + 1, 0)
                    if kt == STEPS - AHEAD + 2 and ahead:
                        take_peak(n + 1)

            take_peak(0)
            exp(0, 0)
            head(0, first=True)
            with act.Fori(1, NHEAD - 1) as n:
                head(n)
            head(NHEAD - 1, ahead=False, more=False)
            take_att(NHEAD - 1)

            act.wait_ge(att_ok, NHEAD)
            def copy_o(g):
                at_least(act, o_turned, KT * g)
                for t in range(TPC):
                    last = act.activation(o_in[:, t, :].rearrange("p (h d) -> p h d", h=HEADS),
                                          vo[:, bass.ds((g // CPB) * HEADS, HEADS),
                                             bass.ds((g % CPB) * TPC + t, 1), :].rearrange("p h o d -> p h (o d)"),
                                          ACT.Copy)
                last.then_inc(o_copied, 1)

            copy_o(0)
            with act.Fori(1, CHUNKS) as g:
                copy_o(g)

        @block.vector
        def _(dve):
            count = [0]

            def link(ins):
                count[0] += 1
                ins.then_inc(setup_step, 1)
                dve.wait_ge(setup_step, count[0])

            dve.memset(eps_col[:, :], EPS)
            dve.memset(all_ones, 1.0)
            link(dve.memset(delta[:, :], 0.0))
            link(dve.memset(delta_rev[:, :], 0.0))
            dve.wait_ge(w_loaded, 16 * LOADS)
            link(dve.tensor_scalar(scale[:, :], scale[:, :], 0.1, 10.0, ALU.max, ALU.min))
            link(dve.tensor_scalar(scale[:, :], scale[:, :], float(EMB) ** 0.5, None, ALU.mult))
            link(dve.reciprocal(scale[:, :], scale[:, :]))
            for t in range(HT):
                last = dve.scalar_tensor_tensor(out=hid[:, t, 0:EMB], in0=w1_raw[:, t, :], scalar=-1.0, in1=w1_raw[:, t, :],
                                                op0=ALU.mult, op1=ALU.max)
            link(last)
            link(dve.tensor_reduce(alpha1[:, :], hid[:, :, 0:EMB], AX.X, ALU.add))
            link(dve.tensor_scalar(alpha1[:, :], alpha1[:, :], 1.0 / EMB, None, ALU.mult))
            link(dve.scalar_tensor_tensor(out=sgn_pos, in0=exps[:, 1], scalar=-1.0, in1=exps[:, 1],
                                          op0=ALU.mult, op1=ALU.max))
            link(dve.tensor_reduce(alpha2[:, :], sgn_pos.rearrange("p (t c) -> p t c", t=KT), AX.X, ALU.add))
            link(dve.tensor_scalar(alpha2[:, :], alpha2[:, :], 1.0 / HIDDEN, None, ALU.mult))
            dve.wait_ge(ident_ok, 2)
            for k in range(KT):
                last = dve.tensor_scalar(diag[:, k], ident[:, :], alpha2[:, k:k + 1], None, ALU.mult)
            link(last)
            dve.engine_nop().then_inc(alpha2_turned, 1)
            for raw, dst in ((exps[:, 0], sgn_pos), (exps[:, 1], sgn_neg)):
                link(dve.tensor_scalar(dst, raw, 0.0, None, ALU.is_gt))
                link(dve.tensor_scalar(raw, raw, 0.0, None, ALU.is_lt))
                link(dve.tensor_tensor(dst, dst, raw, ALU.subtract))
            dve.engine_nop().then_inc(signs_ok, 1)
            dve.wait_ge(table_turned, 1)
            link(dve.tensor_copy(table_t[:, 0:TABLE], ps[0:HEADS, 7, 0:TABLE]))
            link(dve.tensor_scalar(delta[:, 0:TABLE], table_t[:, 0:TABLE], table_t[:, TABLE - 1:TABLE],
                                   scale[0:HEADS, 0:1], ALU.subtract, ALU.mult))
            link(dve.tensor_copy(delta_rev[:, 0:REV + 1], delta[:, REV::-1]))
            dve.engine_nop().then_inc(delta_ok, 1)
            dve.wait_ge(alpha2_turned, 2)
            link(dve.tensor_copy(alpha2_row[:, :], ps[:, 6, 0:EMB]))
            link(dve.tensor_tensor(b2_row[:, :], b2_row[:, :], bp_row[:, :], ALU.add))
            dve.engine_nop().then_inc(consts, 1)

            def layernorm(c, steps):
                dve.wait_ge(x_loaded, 16 * (c + 1))
                slot = bass.ds(c % 2, 1)
                for t in range(TPC):
                    last = dve.bn_stats(stats[:, t, :], x_in[:, slot, t, :].rearrange("p a c -> p (a c)"))
                    last.then_inc(ln_step, 1)
                dve.wait_ge(ln_step, steps + TPC)
                dve.memset(wait_here[:, :], 0.0)
                for t in range(TPC):
                    last = dve.bn_aggr(moments[:, t, :], stats[:, t, :])
                last.then_inc(var_ok, 1)
                dve.wait_ge(std_ok, c + 1)
                dve.reciprocal(rstd[:, :], std[:, :]).then_inc(ln_step, 1)
                dve.wait_ge(ln_step, steps + TPC + 1)
                at_least(dve, xt_turned, KT * c)
                for t in range(TPC):
                    last = dve.tensor_scalar(xn[:, t, :], x_in[:, slot, t, :].rearrange("p a c -> p (a c)"),
                                             moments[:, t, 0:1], rstd[:, t:t + 1], ALU.subtract, ALU.mult)
                last.then_inc(xn_ok, 1)

            LN_STEPS = TPC + 1

            def split_xt(c):
                at_least(dve, h_ready, HT * c)
                done = 3 * c
                for k in range(KT):
                    dve.wait_ge(xt_ok, KT * c + k + 1)
                    dve.tensor_copy(xt_parts[:, 0, k, :], xt[:, k, :]).then_inc(xt_step, 1)
                    dve.wait_ge(xt_step, 3 * (KT * c + k) + 1)
                    dve.tensor_tensor(xt_rest[:, k, :], xt[:, k, :], xt_parts[:, 0, k, :], ALU.subtract).then_inc(xt_step, 1)
                    dve.wait_ge(xt_step, 3 * (KT * c + k) + 2)
                    dve.tensor_copy(xt_parts[:, 1, k, :], xt_rest[:, k, :]).then_inc(xt_step, 1)
                    dve.wait_ge(xt_step, 3 * (KT * c + k) + 3)
                    dve.tensor_tensor(xt_parts[:, 2, k, :], xt_rest[:, k, :], xt_parts[:, 1, k, :],
                                      ALU.subtract).then_inc(xt_parts_ok, 1)

            def take_qkv(c):
                for i in range(ITEMS + 2):
                    dve.wait_ge(qkv_ready, 6 * c + i + 1)
                    src = ps[:, 2 + i % 4, :]
                    if i < ITEMS:
                        at_least(dve, split_ok, ITEMS * c + i - 1)
                        b = (bq_col if i < KT else bk_col)[:, i % KT:i % KT + 1]
                        if i < KT:
                            dve.tensor_scalar(qk_val[:, i % 2, :], src, b, scale[:, 0:1], ALU.add,
                                              ALU.mult).then_inc(qkv_taken, 1)
                        else:
                            dve.tensor_scalar(qk_val[:, i % 2, :], src, b, None, ALU.add).then_inc(qkv_taken, 1)
                    else:
                        for t in range(2):
                            kt = (c % CPB) * TPC + 2 * (i - ITEMS) + t
                            last = dve.tensor_tensor(
                                vo[:, bass.ds((c // CPB) * HEADS, HEADS), bass.ds(kt, 1), :].rearrange("p h o d -> p h (o d)"),
                                src[:, t * EMB:(t + 1) * EMB].rearrange("p (h d) -> p h d", h=HEADS),
                                bv_row[:, :].rearrange("p (h d) -> p h d", h=HEADS), ALU.add)
                        last.then_inc(qkv_taken, 1)

            def take_y(c):
                at_least(dve, base_stored, 16 * c)
                for j in range(2):
                    dve.wait_ge(y_ready, 2 * c + j + 1)
                    dve.tensor_tensor(base[:, 2 * j:2 * j + 2, :], ps[:, 6 + j, :].rearrange("p (t c) -> p t c", t=2),
                                      alpha2_row[:, None, :].to_broadcast([P, 2, EMB]), ALU.mult).then_inc(y_taken[j], 1)

            dve.wait_ge(delta_stored, 32)
            layernorm(0, 0)
            split_xt(0)
            take_qkv(0)
            layernorm(1, LN_STEPS)
            def chunk(c):
                split_xt(c)
                take_y(c - 1)
                take_qkv(c)
                layernorm(c + 1, LN_STEPS * (c + 1))

            chunk(1)
            with dve.Fori(2, CHUNKS - 1) as c:
                chunk(c)
            split_xt(CHUNKS - 1)
            take_y(CHUNKS - 2)
            take_qkv(CHUNKS - 1)
            take_y(CHUNKS - 1)
            dve.memset(v_ones[:, :, HDIM:VCOLS], 1.0).then_inc(ones_ok, 1)
            dve.memset(k_stack[SROWS:MROWS, :, :], 1.0).then_inc(ones_ok, 1)

            def units(n, s, early=False, first_unit=0):
                if s == 0:
                    at_least(dve, peak_ok, n)
                for u in range(UNITS):
                    dve.wait_ge(unit_ready, ALL_UNITS * n + UNITS * s + u + 1)
                    src = ps[:, bank_at(place_of(first_unit + u, early)), :]
                    if s < 4 and u == UNITS - 1:
                        if s == 0:
                            dve.wait_ge(bias_max_loaded, 16 * (n + 1))
                        top = P * s + CHUNK - 1
                        stop = top - CHUNK
                        dve.memset(wait_here[:, :], 0.0)
                        rev = bias_max[:, top:(stop if stop >= 0 else None):-1]
                        dve.tensor_tensor_reduce(out=src, in0=src, in1=rev, scale=1.0, scalar=-3.0e38,
                                                 op0=ALU.add, op1=ALU.max,
                                                 accum_out=peaks[:, s, u:u + 1]).then_inc(unit_done, 1)
                    else:
                        dve.tensor_reduce(peaks[:, s, u:u + 1], src, AX.X, ALU.max).then_inc(unit_done, 1)

            def take_max(n):
                dve.wait_ge(unit_done, 64 * (n + 1))
                at_least(dve, peak_split, n)
                dve.tensor_reduce(peak[:, :], peaks[:, :, :], AX.X, ALU.max).then_inc(peak_ok, 1)

            def bias_scores(n, kt):
                t = kt - (QT - 4)
                if t == 0:
                    dve.wait_ge(bias_exp_loaded, 16 * (n + 1))
                dve.wait_ge(scores_ready[0], QT * n + kt + 1)
                width = P * (t + 1)
                dve.tensor_tensor(ps[:, 0, 0:width], ps[:, 0, 0:width], bias_exp[:, width - 1::-1],
                                  ALU.add).then_inc(scores_biased, 1)

            def normalise(n):
                dve.wait_ge(att_turned, n + 1)
                att = ps[:, bank_at(ATT_PLACE), :].rearrange("p (t c d) -> p t c d", t=TPC, c=CPB)
                dve.reciprocal(rden[:, :, :], att[:, :, :, HDIM]).then_inc(rden_ok, 1)
                dve.wait_ge(rden_ok, n + 1)
                dst = vo[:, bass.ds(n, 1), :, :].rearrange("p n (c t) d -> p t (n c) d", t=TPC)
                for t in range(TPC):
                    last = dve.tensor_tensor(dst[:, t], att[:, t, :, 0:HDIM],
                                             rden[:, t, :, None].to_broadcast([P, CPB, HDIM]), ALU.mult)
                last.then_inc(att_ok, 1)

            def head(n, first=False, ahead2=True, ahead1=True):
                for kt in range(1, STEPS + 1):
                    if QT - 4 <= kt < STEPS:
                        bias_scores(n, kt)
                    if kt == 2 and not first:
                        normalise(n - 1)
                    if kt <= STEPS - AHEAD:
                        if ahead1:
                            units(n + 1, kt + AHEAD - 1, False, UNITS * (kt - 1))
                            if kt == STEPS - AHEAD:
                                take_max(n + 1)
                    elif ahead2:
                        units(n + 2, kt - (STEPS - AHEAD) - 1, False, UNITS * (kt - 1))
            for s in range(STEPS):
                units(0, s, True, UNITS * s)
            take_max(0)
            for s in range(AHEAD):
                units(1, s, True, ALL_UNITS + UNITS * s)
            head(0, first=True)
            with dve.Fori(1, NHEAD - 2) as n:
                head(n)
            head(NHEAD - 2, ahead2=False)
            head(NHEAD - 1, ahead2=False, ahead1=False)
            normalise(NHEAD - 1)

            def sum_out(r):
                for i in range(2):
                    g = 2 * r + i
                    at_least(dve, proj_ready, 2 * g)
                    for k in range(KT):
                        dve.wait_ge(o_turned, KT * g + k + 1)
                        dve.tensor_copy(o_t[:, k, :], ps[:, k, :]).then_inc(ot_ok[k], 1)
                    dve.wait_ge(base_loaded[i], 16 * (r + 1))
                    for j in range(2):
                        dve.wait_ge(proj_ready, 2 * g + j + 1)
                        dst = base_in[:, i, 2 * j:2 * j + 2, :].rearrange("p t c -> p (t c)")
                        last = dve.tensor_tensor(dst, ps[:, 2 + j, :], dst, ALU.add)
                    last.then_inc(out_ok, 1)

            sum_out(0)
            with dve.Fori(1, CHUNKS // 2) as r:
                sum_out(r)

        @block.gpsimd
        def _(pool):
            def convert(out, in_):
                shape = list(in_.shape)
                zero = zeros[:, 0:1] if len(shape) == 2 else zeros[:, None, 0:1]
                return pool.tensor_tensor(out, in_, zero.to_broadcast(shape), ALU.add)

            for m in (ident, ident16):
                pool.memset(m[:, :], 0.0).then_inc(split_step, 1)
            pool.memset(peak_parts[:], 0.0).then_inc(ones_ok, 1)
            pool.memset(zeros[:, :], 0.0).then_inc(split_step, 1)
            pool.wait_ge(split_step, 3)
            for m in (ident, ident16):
                pool.affine_select(out=m[:, :], in_=m[:, :], compare_op=ALU.not_equal, fill=1.0, base=0,
                                   pattern=[[-1, P]], channel_multiplier=1).then_inc(ident_ok, 1)
            pool.wait_ge(consts, 1)

            def add_base(c):
                slot = bass.ds(c % 2, 1)
                for j in range(2):
                    pool.wait_ge(y_taken[j], c + 1)
                pool.tensor_tensor(base[:], base[:], x_in[:, slot].rearrange("p a t c -> p (a t) c"),
                                   ALU.add).then_inc(base_step, 1)
                pool.wait_ge(base_step, c + 1)
                pool.tensor_tensor(base[:], base[:], b2_row[:, None, :].to_broadcast([P, TPC, EMB]),
                                   ALU.add).then_inc(base_ok, 1)

            def split_qk(c):
                for i in range(ITEMS):
                    at = ITEMS * c + i
                    s = i % 2
                    done = 3 + 3 * at
                    pool.wait_ge(qkv_taken, 6 * c + i + 1)
                    at_least(pool, part_stored[s], 16 * (2 * c + i // 2))
                    convert(qk_part[:, s, 0, :], qk_val[:, s, :]).then_inc(split_step, 1)
                    pool.wait_ge(split_step, done + 1)
                    pool.tensor_tensor(qk_rest[:, s, :], qk_val[:, s, :], qk_part[:, s, 0, :],
                                       ALU.subtract).then_inc(split_step, 1)
                    pool.wait_ge(split_step, done + 2)
                    convert(qk_part[:, s, 1, :], qk_rest[:, s, :]).then_inc(split_step, 1)
                    pool.wait_ge(split_step, done + 3)
                    pool.tensor_tensor(qk_part[:, s, 2, :], qk_rest[:, s, :], qk_part[:, s, 1, :],
                                       ALU.subtract).then_inc(split_ok, 1)

            split_qk(0)
            with pool.Fori(1, CHUNKS) as c:
                add_base(c - 1)
                split_qk(c)
            add_base(CHUNKS - 1)

            def copy_v(n, part):
                at_least(pool, pv_done, QT * n - (8 if part == 0 else 0))
                rows = slice(8 * part, 8 * part + 8)
                convert(v_ones[:, rows, 0:HDIM],
                                 vo[:, bass.ds(n, 1), rows, :].rearrange("p n t d -> p (n t) d")).then_inc(v_copied, 1)

            def split_peak(n):
                pool.wait_ge(peak_ok, n + 1)
                at_least(pool, peak_turned, n)
                steps = 4 * n
                pool.tensor_tensor(neg_peak[:, 0, :], zeros[:, :], peak[:, :], ALU.subtract).then_inc(peak_step, 1)
                pool.wait_ge(peak_step, steps + 1)
                convert(peak_parts[:, 0, :], neg_peak[:, 0, :]).then_inc(peak_step, 1)
                pool.wait_ge(peak_step, steps + 2)
                pool.tensor_tensor(neg_peak[:, 1, :], neg_peak[:, 0, :], peak_parts[:, 0, :],
                                   ALU.subtract).then_inc(peak_step, 1)
                pool.wait_ge(peak_step, steps + 3)
                convert(peak_parts[:, 1, :], neg_peak[:, 1, :]).then_inc(peak_step, 1)
                pool.wait_ge(peak_step, steps + 4)
                pool.tensor_tensor(peak_parts[:, 2, :], neg_peak[:, 1, :], peak_parts[:, 1, :],
                                   ALU.subtract).then_inc(peak_split, 1)

            pool.wait_ge(qkv_taken, 6 * CHUNKS)
            copy_v(0, 0)
            copy_v(0, 1)
            split_peak(0)
            with pool.Fori(1, NHEAD) as n:
                copy_v(n, 0)
                split_peak(n)
                copy_v(n, 1)


_INS = ['L0_attn_x', 'L0_attn_Wq', 'L0_attn_bq', 'L0_attn_Wk', 'L0_attn_bk', 'L0_attn_Wv', 'L0_attn_bv', 'L0_attn_Wp',
        'L0_attn_bp', 'L0_attn_bias_table', 'L0_attn_temperature', 'L0_ffn_w1', 'L0_ffn_b1', 'L0_ffn_w2', 'L0_ffn_b2']


def kernel(**inputs):
    import numpy as _np
    import concourse.bacc as _bacc
    from concourse import mybir as _mybir
    from concourse.bass_utils import run_bass_kernel_spmd as _run

    nc = _bacc.Bacc("TRN2", target_bir_lowering=False, num_devices=1)
    arrays, args = {}, []
    for name in _INS:
        a = _np.ascontiguousarray(inputs[name])
        arrays[f"in_{name}_dram"] = a
        args.append(nc.dram_tensor(f"in_{name}_dram", a.shape, _mybir.dt.from_np(a.dtype), kind="ExternalInput").ap())
    args.append(nc.dram_tensor("out_0_dram", (BATCH, TOKENS, EMB), F32, kind="ExternalOutput").ap())
    build(nc, *args)
    r = _run(nc, [arrays], core_ids=[0])
    return r.results[0]["out_0_dram"]
```

```python
from contextlib import ExitStack

import concourse.bass as bass
from concourse import mybir

ALU = mybir.AluOpType
ACT = mybir.ActivationFunctionType
AX = mybir.AxisListType
F32 = mybir.dt.float32
BF16 = mybir.dt.bfloat16
F16 = mybir.dt.float16

P = 128
BATCH, TOKENS, EMB = 4, 2048, 256
HEADS = 16
HDIM = EMB // HEADS
HIDDEN = 1024
TABLE = 499
EPS = 1e-5

KT = EMB // P
HT = HIDDEN // P
CHUNK = 512
TPC = CHUNK // P
CHUNKS = BATCH * TOKENS // CHUNK
CPB = TOKENS // CHUNK
NHEAD = BATCH * HEADS
QT = TOKENS // P
PARTS = 3
PAIRS = 6
SROWS = PAIRS * HDIM
MROWS = SROWS + PARTS
SLOTS = 3
VCOLS = 32
STEPS = QT
HALVES = 2
AHEAD = 4
FIRST_KEY = TOKENS - CHUNK
ORDER = "0m1m2v3"
WWIDE = CHUNK + 3 * P
REV = CHUNK + P - 2
DELTA = 1024
ITEMS = 2 * KT
LOW = 2.0 ** 11
X_SLOTS = 3
MADE = [("q", 0), ("q", 1), ("v", 0), ("v", 1), ("k", 0), ("k", 1)]
SPLIT = [i for i, (what, _) in enumerate(MADE) if what != "v"]


TURN_BANKS = (0, 1, 2)
ATT_BANK = 3
MAX_BANKS = (4, 6)
ALL_CHUNKS = QT * CPB
ALL_UNITS = QT * HALVES
ATT_STEP, PEAK_STEP = 3, STEPS - AHEAD + 2
ATT_AT, PEAK_AT = CPB * (ATT_STEP - 1), CPB * (PEAK_STEP - 1)


def place_of(chunk):
    return chunk + (chunk >= ATT_AT) + (chunk >= PEAK_AT)


ATT_PLACE, PEAK_PLACE, FIRST_PEAK_PLACE = ATT_AT, PEAK_AT + 1, -1 - CPB
CHUNK_AT = {place_of(c): c for c in range(-CPB, ALL_CHUNKS)}


def bank_at(place):
    return TURN_BANKS[place % 3]


def high_half(x):
    v = x.bitcast(BF16)
    return v[(slice(None),) * (len(v.shape) - 1) + (slice(1, None, 2),)]


def at_least(engine, sem, value):
    if isinstance(value, int) and value <= 0:
        return
    engine.wait_ge(sem, value)


def build(nc, x, wq, bq, wk, bk, wv, bv, wp, bp, table, temperature, w1, b1, w2, b2, out):
    with ExitStack() as ctx:
        def sb(name, shape, dt=F32):
            return ctx.enter_context(nc.sbuf_tensor(name, shape, dt))

        def sem(name):
            return ctx.enter_context(nc.semaphore(name))

        parts_dram = nc.dram_tensor("parts_dram", [2, PARTS, BATCH * EMB, TOKENS], BF16).ap()
        base_dram = nc.dram_tensor("base_dram", [BATCH * TOKENS, EMB], F32).ap()
        delta_dram = nc.dram_tensor("delta_dram", [2, HEADS, DELTA], F32).ap()

        ident = sb("ident", [P, P])
        ident16 = sb("ident16", [P, P], BF16)
        scale = sb("scale", [P, 1])
        wproj = sb("wproj", [P, KT, EMB])
        vo = sb("vo", [P, NHEAD, QT, HDIM])

        wq_sb = sb("wq_sb", [P, KT, EMB])
        wk_sb = sb("wk_sb", [P, KT, EMB])
        wv_sb = sb("wv_sb", [P, KT, EMB])
        sign1 = sb("sign1", [P, KT, HIDDEN], F16)
        sign1_low = sb("sign1_low", [P, KT, HIDDEN], F16)
        sign2 = sb("sign2", [P, HT, EMB], BF16)
        alpha1 = sb("alpha1", [P, HT])
        alpha2 = sb("alpha2", [P, KT])
        alpha2_row = sb("alpha2_row", [P, EMB])
        bq_col = sb("bq_col", [P, KT])
        bk_col = sb("bk_col", [P, KT])
        b1_col = sb("b1_col", [P, HT])
        bv_row = sb("bv_row", [P, EMB])
        b2_row = sb("b2_row", [P, EMB])
        x_in = sb("x_in", [P, X_SLOTS, TPC, EMB])
        stats = sb("stats", [P, TPC, 6])
        wait_here = sb("wait_here", [P, 1])
        moments = sb("moments", [P, TPC, 2])
        std = sb("std", [P, TPC])
        rstd = sb("rstd", [P, TPC])
        eps_col = sb("eps_col", [P, 1])
        xn = sb("xn", [P, TPC, EMB])
        xt = sb("xt", [P, KT, CHUNK])
        xt_rest = sb("xt_rest", [P, KT, CHUNK])
        xt_high = sb("xt_high", [P, KT, CHUNK], F16)
        xt_low = sb("xt_low", [P, KT, CHUNK], F16)
        hid = sb("hid", [P, HT, CHUNK])
        hid_low = sb("hid_low", [P, HT, CHUNK], BF16)
        qk_val = sb("qk_val", [P, 2, CHUNK])
        qk_rest = sb("qk_rest", [P, 2, CHUNK])
        qk_part = sb("qk_part", [P, 2, PARTS, CHUNK], BF16)
        base = sb("base", [P, TPC, EMB])

        stack_room = sb("stack_room", [P, 2, SLOTS, TOKENS], BF16)
        q_stack = stack_room[:, 0]
        k_stack = stack_room[:, 1]
        exps = sb("exps", [P, 2, TOKENS])
        v_ones = sb("v_ones", [P, QT, VCOLS])
        bias_max = xn[:].rearrange("p t c -> p (t c)")[:, 0:WWIDE]
        bias_exp = xt[:, 0]
        peaks = sb("peaks", [P, QT, CPB])
        peak = sb("peak", [P, QT])
        zeros = sb("zeros", [P, QT])
        neg_peak = sb("neg_peak", [P, 2, QT])
        peak_parts = sb("peak_parts", [P, P // QT, QT], BF16)
        peak_rows = sb("peak_rows", [PARTS * QT, P], BF16)
        att_t = xt_rest[:, 0]
        rden = sb("rden", [P, TPC, CPB])

        hid_rest = exps[:].rearrange("p a (b c) -> p (a b) c", c=CHUNK)
        room = stack_room[:].rearrange("p a s t -> p (a s t)").bitcast(F32)
        w1_raw = exps[:, 0].rearrange("p (t c) -> p t c", t=HT)
        w2_raw = exps[:, 1].rearrange("p (t c) -> p t c", t=KT)
        sgn_pos = hid[:, 0:4].rearrange("p a b -> p (a b)")
        sgn_neg = hid[:, 4:8].rearrange("p a b -> p (a b)")
        table_in = room[:, 4 * DELTA:4 * DELTA + 4 * HEADS].rearrange("p (t h) -> p t h", t=4)
        table_t = room[0:HEADS, 0:DELTA]
        delta = room[0:HEADS, DELTA:2 * DELTA]
        delta_rev = room[0:HEADS, 2 * DELTA:3 * DELTA]
        bp_row = room[:, 5 * DELTA:5 * DELTA + EMB]
        diag = base[:, 0:KT, 0:P]
        all_ones = base[:, KT, 0:P]
        o_in = xn
        o_t = xt
        base_in = x_in

        ps = ctx.enter_context(nc.psum_tensor("ps", [P, 8, CHUNK], F32))

        w_loaded = sem("w_loaded")
        consts = sem("consts")
        ident_ok = sem("ident_ok")
        setup_step = sem("setup_step")
        signs_ok = sem("signs_ok")
        alpha2_turned = sem("alpha2_turned")
        sign_turned = sem("sign_turned")
        sign_copied = sem("sign_copied")
        table_turned = sem("table_turned")
        delta_ok = sem("delta_ok")
        delta_stored = sem("delta_stored")
        x_loaded = sem("x_loaded")
        ln_step = sem("ln_step")
        var_ok = sem("var_ok")
        std_ok = sem("std_ok")
        xn_ok = sem("xn_ok")
        xt_turned = sem("xt_turned")
        xt_ok = sem("xt_ok")
        xt_step = sem("xt_step")
        xt_parts_ok = sem("xt_parts_ok")
        hid_step = sem("hid_step")
        hid_parts_ok = sem("hid_parts_ok")
        qkv_ready = sem("qkv_ready")
        qkv_taken = sem("qkv_taken")
        h_ready = sem("h_ready")
        h_taken = sem("h_taken")
        y_ready = sem("y_ready")
        y_taken = [sem("y_taken0"), sem("y_taken1")]
        split_step = sem("split_step")
        split_ok = sem("split_ok")
        base_step = sem("base_step")
        base_ok = sem("base_ok")
        base_stored = sem("base_stored")
        part_stored = [sem("part_stored0"), sem("part_stored1")]
        stack_loaded = sem("stack_loaded")
        bias_max_loaded = sem("bias_max_loaded")
        bias_exp_loaded = sem("bias_exp_loaded")
        ones_ok = sem("ones_ok")
        unit_ready = sem("unit_ready")
        unit_done = sem("unit_done")
        peak_ok = sem("peak_ok")
        peak_step = sem("peak_step")
        peak_split = sem("peak_split")
        peak_turned = sem("peak_turned")
        peak_copied = sem("peak_copied")
        peak_loaded = sem("peak_loaded")
        scores_ready = sem("scores_ready")
        scores_biased = sem("scores_biased")
        exp_done = sem("exp_done")
        v_copied = sem("v_copied")
        pv_done = sem("pv_done")
        att_copied = sem("att_copied")
        att_turned = sem("att_turned")
        rden_ok = sem("rden_ok")
        att_ok = sem("att_ok")
        base_loaded = [sem("base_loaded0"), sem("base_loaded1")]
        o_copied = sem("o_copied")
        o_turned = sem("o_turned")
        ot_ok = [sem("ot_ok0"), sem("ot_ok1")]
        proj_ready = sem("proj_ready")
        out_ok = sem("out_ok")
        out_stored = [sem("out_stored0"), sem("out_stored1")]

        x_rows = x.rearrange("b (g t p) c -> p (b g) t c", t=TPC, p=P)
        out_rows = out.rearrange("b (g t p) c -> p (b g) t c", t=TPC, p=P)
        base_rows = base_dram.rearrange("(g t p) c -> p g t c", t=TPC, p=P)

        LOADS = 15
        TURNS = 2 * HT * KT

        block = ctx.enter_context(nc.Block())

        @block.sync
        def _(sp):
            def row(v):
                return bass.AP(tensor=v.tensor, offset=v.offset, ap=[[0, P], [1, v.shape[0]]])

            def weight(w):
                return w.rearrange("(t p) c -> p t c", p=P)

            sp.dma_start(x_in[:, 0], x_rows[:, 0]).then_inc(x_loaded, 16)
            sp.dma_start(w1_raw, w1.rearrange("(t p) c -> p t c", p=P)).then_inc(w_loaded, 16)
            sp.dma_start(w2_raw, w2.rearrange("(t p) c -> p t c", p=P)).then_inc(w_loaded, 16)
            sp.dma_start(table_in[:, 0:3], table[0:3 * P, :].rearrange("(t p) h -> p t h", p=P)).then_inc(w_loaded, 16)
            sp.dma_start(table_in[0:TABLE - 3 * P, 3], table[3 * P:TABLE, :]).then_inc(w_loaded, 16)
            sp.dma_start(scale[:, :], row(temperature)).then_inc(w_loaded, 16)
            sp.dma_start(b1_col[:, :], b1.rearrange("(t p) -> p t", p=P),
                         allow_slow_non_contiguous=True).then_inc(w_loaded, 16)
            sp.dma_start(bq_col[:, :], bq.rearrange("(t p) -> p t", p=P),
                         allow_slow_non_contiguous=True).then_inc(w_loaded, 16)
            sp.dma_start(bk_col[:, :], bk.rearrange("(t p) -> p t", p=P),
                         allow_slow_non_contiguous=True).then_inc(w_loaded, 16)
            sp.dma_start(bv_row[:, :], row(bv)).then_inc(w_loaded, 16)
            sp.dma_start(b2_row[:, :], row(b2)).then_inc(w_loaded, 16)
            sp.dma_start(bp_row[:, :], row(bp)).then_inc(w_loaded, 16)
            sp.dma_start(wq_sb[:], weight(wq)).then_inc(w_loaded, 16)
            sp.dma_start(wk_sb[:], weight(wk)).then_inc(w_loaded, 16)
            sp.dma_start(wv_sb[:], weight(wv)).then_inc(w_loaded, 16)
            sp.dma_start(wproj[:], weight(wp)).then_inc(w_loaded, 16)
            sp.wait_ge(delta_ok, 1)
            sp.dma_start(delta_dram[0], delta).then_inc(delta_stored, 16)
            sp.dma_start(delta_dram[1], delta_rev).then_inc(delta_stored, 16)
            sp.wait_ge(delta_stored, 32)

            def load_x(c):
                sp.wait_ge(x_loaded, 16 * c)
                sp.dma_start(x_in[:, bass.ds(c % X_SLOTS, 1)], x_rows[:, bass.ds(c, 1)]).then_inc(x_loaded, 16)

            def store_parts(c):
                rows = (c // CPB) * EMB
                cols = (c % CPB) * CHUNK
                for i in range(ITEMS):
                    sp.wait_ge(split_ok, ITEMS * c + i + 1)
                    dst = parts_dram[i // KT, :, bass.ds(rows + (i % KT) * P, P), bass.ds(cols, CHUNK)]
                    sp.dma_start(dst.rearrange("a r c -> r a c"), qk_part[:, i % 2]).then_inc(part_stored[i % 2], 16)

            def store_base(c):
                sp.wait_ge(base_ok, c + 1)
                sp.dma_start(base_rows[:, bass.ds(c, 1)], base[:]).then_inc(base_stored, 16)

            load_x(1)
            load_x(2)
            store_parts(0)
            with sp.Fori(1, CHUNKS - 2) as c:
                store_parts(c)
                store_base(c - 1)
                load_x(c + 2)
            for c in range(CHUNKS - 2, CHUNKS):
                store_parts(c)
                store_base(c - 1)
            store_base(CHUNKS - 1)
            for i in range(2):
                sp.wait_ge(part_stored[i], 16 * 2 * CHUNKS)
            sp.wait_ge(base_stored, 16 * CHUNKS)

            def load_stack(n):
                slot = n % SLOTS
                at_least(sp, stack_loaded, 16 * 12 * n)
                at = 0
                for a in range(PARTS):
                    k = PARTS - a
                    for j in range(k):
                        sp.dma_start(q_stack[at + j * HDIM:at + (j + 1) * HDIM, bass.ds(slot, 1), :],
                                     parts_dram[0, a, bass.ds(n * HDIM, HDIM), :]).then_inc(stack_loaded, 16)
                    for j in range(k):
                        sp.dma_start(k_stack[at + j * HDIM:at + (j + 1) * HDIM, bass.ds(slot, 1), :],
                                     parts_dram[1, j, bass.ds(n * HDIM, HDIM), :]).then_inc(stack_loaded, 16)
                    at += k * HDIM

            def toeplitz(which, n, width):
                r = delta_dram[which, bass.ds(n % HEADS, 1), 0:width]
                return bass.AP(tensor=r.tensor, offset=r.offset, ap=[[1, P], [1, width]])

            def load_bias_max(n):
                if not isinstance(n, int) or n > 0:
                    sp.wait_ge(unit_done, ALL_UNITS * (n - 1) + 4 * HALVES)
                sp.dma_start(bias_max[:, :], toeplitz(0, n, WWIDE)).then_inc(bias_max_loaded, 16)

            def load_bias_exp(n):
                at_least(sp, scores_biased, 4 * n)
                sp.dma_start(bias_exp[:, :], toeplitz(1, n, CHUNK)).then_inc(bias_exp_loaded, 16)

            def load_peak(n):
                sp.wait_ge(peak_copied, n + 1)
                dst = q_stack[SROWS:MROWS, bass.ds(n % SLOTS, 1), :].rearrange("a s (t p) -> a (s t) p", p=P)
                sp.dma_start(dst, peak_rows[:, :]).then_inc(peak_loaded, 16)

            load_stack(0)
            load_bias_max(0)
            load_stack(1)
            load_bias_max(1)
            load_peak(0)

            def head_loads(n, stack=True, peaks_too=True):
                if stack:
                    at_least(sp, scores_ready, ALL_CHUNKS * n)
                    load_stack(n + 2)
                load_bias_exp(n)
                if stack:
                    load_bias_max(n + 2)
                if peaks_too:
                    load_peak(n + 1)

            head_loads(0)
            with sp.Fori(1, NHEAD - 2) as n:
                head_loads(n)
            head_loads(NHEAD - 2, stack=False)
            head_loads(NHEAD - 1, stack=False, peaks_too=False)

            def load_base(g, j):
                sp.dma_start(base_in[:, j], base_rows[:, bass.ds(g, 1)]).then_inc(base_loaded[j], 16)

            def store_out(g, j):
                sp.wait_ge(out_ok, g + 1)
                sp.dma_start(out_rows[:, bass.ds(g, 1)], base_in[:, j]).then_inc(out_stored[j], 16)

            load_base(0, 0)
            load_base(1, 1)
            with sp.Fori(0, CHUNKS // 2 - 1) as r:
                for j in range(2):
                    store_out(2 * r + j, j)
                    sp.wait_ge(out_stored[j], 16 * (r + 1))
                    load_base(2 * r + j + 2, j)
            for j in range(2):
                store_out(CHUNKS - 2 + j, j)
            for j in range(2):
                sp.wait_ge(out_stored[j], 16 * (CHUNKS // 2))

        @block.tensor
        def _(pe):
            pe.wait_ge(ident_ok, 2)
            pe.wait_ge(w_loaded, 16 * LOADS)
            for t in range(4):
                rows = P if t < 3 else TABLE - 3 * P
                last = pe.transpose(ps[0:HEADS, 7, t * P:t * P + rows], table_in[0:rows, t, :], ident[0:rows, 0:rows])
            last.then_inc(table_turned, 1)
            def turn_x(c):
                pe.wait_ge(xn_ok, c + 1)
                for k in range(KT):
                    at_least(pe, xt_ok, KT * c - KT + k + 1)
                    for t in range(TPC):
                        last = pe.transpose(ps[:, k, t * P:(t + 1) * P], xn[:, t, k * P:(k + 1) * P], ident[:, :])
                    last.then_inc(xt_turned, 1)

            def qkv(c):
                pe.wait_ge(xt_ok, KT * (c + 1))
                for i, (what, j) in enumerate(MADE):
                    if i < 4:
                        at_least(pe, h_taken, HT * c - 4 + (i + 2) % 4 + 1)
                    else:
                        pe.wait_ge(qkv_taken, 6 * c + i - 3)
                    bank = 2 + i % 4
                    if what != "v":
                        w = wq_sb if what == "q" else wk_sb
                        for k in range(KT):
                            last = pe.matmul(ps[:, bank, :], w[:, k, j * P:(j + 1) * P], xt[:, k, :],
                                             start=(k == 0), stop=(k == KT - 1))
                    else:
                        for t in range(2):
                            tile = 2 * j + t
                            for k in range(KT):
                                last = pe.matmul(ps[:, bank, t * EMB:(t + 1) * EMB], xt[:, k, tile * P:(tile + 1) * P],
                                                 wv_sb[:, k, :], start=(k == 0), stop=(k == KT - 1))
                    last.then_inc(qkv_ready, 1)

            def hidden(c, tiles):
                if tiles[0] == 0:
                    pe.wait_ge(xt_parts_ok, KT * (c + 1))
                for m in tiles:
                    i = len(MADE) + m
                    if m < 4:
                        pe.wait_ge(qkv_taken, 6 * c + i - 3)
                    else:
                        pe.wait_ge(h_taken, HT * c + m - 3)
                    for k in range(KT):
                        cols = slice(m * P, (m + 1) * P)
                        pe.matmul(ps[:, 2 + i % 4, :], sign1[:, k, cols], xt_high[:, k, :],
                                  start=(k == 0), stop=False)
                        last = pe.matmul(ps[:, 2 + i % 4, :], sign1_low[:, k, cols], xt_low[:, k, :],
                                         start=False, stop=(k == KT - 1))
                    last.then_inc(h_ready, 1)

            def ffn_out(c):
                for j in range(2):
                    pe.wait_ge(y_taken[j], c + 1)
                    for t in range(2):
                        tile = 2 * j + t
                        cols = slice(tile * P, (tile + 1) * P)
                        for m in range(HT):
                            if tile == 0:
                                pe.wait_ge(hid_parts_ok, HT * c + m + 1)
                            parts = (high_half(hid[:, m, cols]), high_half(hid_rest[:, m, cols]), hid_low[:, m, cols])
                            for a, h in enumerate(parts):
                                last = pe.matmul(ps[:, 6 + j, t * EMB:(t + 1) * EMB], h, sign2[:, m, :],
                                                 start=(m == 0 and a == 0), stop=(m == HT - 1 and a == PARTS - 1))
                    last.then_inc(y_ready, 1)

            turn_x(0)
            pe.wait_ge(alpha2_turned, 1)
            for k in range(KT):
                last = pe.matmul(ps[:, 6, k * P:(k + 1) * P], all_ones, diag[:, k], start=True, stop=True)
            last.then_inc(alpha2_turned, 1)
            qkv(0)
            pe.wait_ge(signs_ok, 1)
            pe.wait_ge(y_taken[0], 1)
            pe.wait_ge(y_taken[1], 1)
            for b in range(TURNS):
                if b >= 2:
                    pe.wait_ge(sign_copied, b - 1)
                second, t = divmod(b, TURNS // 2)
                src = sgn_pos if not second else sgn_neg
                pe.transpose(ps[:, 6 + b % 2, 0:P], src[:, t * P:(t + 1) * P], ident[:, :]).then_inc(sign_turned, 1)
            pe.wait_ge(sign_copied, TURNS)
            first, second = range(HT // 2), range(HT // 2, HT)
            hidden(0, first)
            turn_x(1)
            hidden(0, second)

            def chunk(c):
                qkv(c)
                ffn_out(c - 1)
                hidden(c, first)
                turn_x(c + 1)
                hidden(c, second)

            with pe.Fori(1, CHUNKS - 1) as c:
                chunk(c)
            qkv(CHUNKS - 1)
            ffn_out(CHUNKS - 2)
            hidden(CHUNKS - 1, range(HT))
            ffn_out(CHUNKS - 1)
            for j in range(2):
                pe.wait_ge(y_taken[j], CHUNKS + 1)
            pe.wait_ge(ones_ok, 3)

            def bank_free(n, place):
                before = place - 3
                first, final = (isinstance(n, int) and n == k for k in (0, NHEAD - 1))
                if before == ATT_PLACE and not first:
                    pe.wait_ge(att_ok, n)
                elif before == PEAK_PLACE and not final:
                    pe.wait_ge(peak_copied, n + 2)
                elif before == FIRST_PEAK_PLACE and first:
                    pe.wait_ge(peak_copied, 1)
                else:
                    if before in (ATT_PLACE, PEAK_PLACE):
                        before -= 3
                    if before >= -CPB:
                        pe.wait_ge(exp_done, ALL_CHUNKS * n + CPB + CHUNK_AT[before] + 1)

            def unit(n, s, half):
                if s == 0 and half == 0:
                    pe.wait_ge(stack_loaded, 16 * 12 * (n + 1))
                at_least(pe, unit_done, ALL_UNITS * n + HALVES * s + half - 1)
                for j in range(2):
                    at = (2 * half + j) * CHUNK
                    last = pe.matmul(ps[:, MAX_BANKS[half] + j, :],
                                     q_stack[0:SROWS, bass.ds(n % SLOTS, 1), s * P:(s + 1) * P],
                                     k_stack[0:SROWS, bass.ds(n % SLOTS, 1), at:at + CHUNK], start=True, stop=True)
                last.then_inc(unit_ready, 1)

            def turn_peak(n, body, place):
                pe.wait_ge(peak_split, n + 1)
                bank_free(body, place)
                pe.transpose(ps[:, bank_at(place), :].bitcast(BF16)[:, 0:P],
                             peak_parts[:].rearrange("p a t -> p (a t)"), ident16[:, :]).then_inc(peak_turned, 1)

            def turn_att(n):
                pe.wait_ge(att_copied, n + 1)
                if isinstance(n, int) and n == NHEAD - 1:
                    pe.wait_ge(exp_done, ALL_CHUNKS * NHEAD)
                    pe.wait_ge(att_ok, n)
                else:
                    bank_free(n + 1, ATT_PLACE)
                for t in range(TPC):
                    last = pe.transpose(ps[:, bank_at(ATT_PLACE), t * P:(t + 1) * P], att_t[:, t * P:(t + 1) * P],
                                        ident[:, :])
                last.then_inc(att_turned, 1)

            def scores(n, kt, c, body, chunk):
                if kt == 0 and c == 0:
                    pe.wait_ge(peak_loaded, 16 * (n + 1))
                bank_free(body, place_of(chunk))
                pe.matmul(ps[:, bank_at(place_of(chunk)), :],
                          k_stack[0:MROWS, bass.ds(n % SLOTS, 1), kt * P:(kt + 1) * P],
                          q_stack[0:MROWS, bass.ds(n % SLOTS, 1), c * CHUNK:(c + 1) * CHUNK],
                          start=True, stop=True).then_inc(scores_ready, 1)

            def times_v(n, kt):
                pe.wait_ge(exp_done, ALL_CHUNKS * n + CPB * (kt + 1))
                if kt % 8 == 0:
                    pe.wait_ge(v_copied, 2 * n + kt // 8 + 1)
                if kt == 0:
                    at_least(pe, att_copied, n)
                for c in range(CPB):
                    last = pe.matmul(ps[c * VCOLS:(c + 1) * VCOLS, ATT_BANK, :], v_ones[:, kt, :],
                                     exps[:, kt % 2, c * CHUNK:(c + 1) * CHUNK], start=(kt == 0), stop=(kt == QT - 1))
                last.then_inc(pv_done, 1)

            def head(n, first=False, ahead2=True, ahead1=True, more=True):
                for kt in range(1, STEPS + 1):
                    if kt == ATT_STEP and not first:
                        turn_att(n - 1)
                    if kt == PEAK_STEP and ahead1:
                        turn_peak(n + 1, n, PEAK_PLACE)
                    half = 0
                    for turn in ORDER:
                        if turn == "m":
                            if kt <= STEPS - AHEAD:
                                if ahead1:
                                    unit(n + 1, kt + AHEAD - 1, half)
                            elif ahead2:
                                unit(n + 2, kt - (STEPS - AHEAD) - 1, half)
                            half += 1
                        elif turn == "v":
                            times_v(n, kt - 1)
                        elif kt < STEPS:
                            scores(n, kt, int(turn), n, CPB * (kt - 1) + int(turn))
                        elif more:
                            scores(n + 1, 0, int(turn), n, CPB * (kt - 1) + int(turn))

            for s in range(STEPS):
                for half in range(HALVES):
                    unit(0, s, half)
            for s in range(AHEAD):
                for half in range(HALVES):
                    unit(1, s, half)
                if s == 0:
                    turn_peak(0, 0, FIRST_PEAK_PLACE)
            for c in range(CPB):
                scores(0, 0, c, 0, c - CPB)
            head(0, first=True)
            with pe.Fori(1, NHEAD - 2) as n:
                head(n)
            head(NHEAD - 2, ahead2=False)
            head(NHEAD - 1, ahead2=False, ahead1=False, more=False)
            turn_att(NHEAD - 1)
            pe.wait_ge(att_ok, NHEAD)

            def turn_o(g):
                pe.wait_ge(o_copied, g + 1)
                for k in range(KT):
                    at_least(pe, ot_ok[k], g)
                    for t in range(TPC):
                        last = pe.transpose(ps[:, k, t * P:(t + 1) * P], o_in[:, t, k * P:(k + 1) * P], ident[:, :])
                    last.then_inc(o_turned, 1)

            def project(g):
                for k in range(KT):
                    pe.wait_ge(ot_ok[k], g + 1)
                for j in range(2):
                    at_least(pe, out_ok, g)
                    for t in range(2):
                        for k in range(KT):
                            tile = 2 * j + t
                            last = pe.matmul(ps[:, 2 + j, t * EMB:(t + 1) * EMB], o_t[:, k, tile * P:(tile + 1) * P],
                                             wproj[:, k, :], start=(k == 0), stop=(k == KT - 1))
                    last.then_inc(proj_ready, 1)

            turn_o(0)
            project(0)
            with pe.Fori(1, CHUNKS) as g:
                turn_o(g)
                project(g)

        @block.scalar
        def _(act):
            def turned_signs(b):
                act.wait_ge(sign_turned, b + 1)
                second, t = divmod(b, TURNS // 2)
                if not second:
                    cols = slice((t // KT) * P, (t // KT + 1) * P)
                    act.activation(sign1_low[:, t % KT, cols], ps[:, 6 + b % 2, 0:P], ACT.Copy, scale=1.0 / LOW)
                    dst = sign1[:, t % KT, cols]
                else:
                    dst = sign2[:, t % HT, (t // HT) * P:(t // HT + 1) * P]
                act.activation(dst, ps[:, 6 + b % 2, 0:P], ACT.Copy).then_inc(sign_copied, 1)

            def root(c):
                act.wait_ge(var_ok, c + 1)
                act.activation(std[:, :], moments[:, :, 1], ACT.Sqrt, bias=eps_col[:, 0:1]).then_inc(std_ok, 1)

            def take_xt(c):
                at_least(act, qkv_ready, 6 * c)
                at_least(act, xt_parts_ok, KT * c)
                for k in range(KT):
                    act.wait_ge(xt_turned, KT * c + k + 1)
                    act.activation(xt[:, k, :], ps[:, k, :], ACT.Copy).then_inc(xt_ok, 1)

            def gelus(c, tiles):
                if tiles[0] == 0:
                    at_least(act, y_ready, 2 * c)
                for m in tiles:
                    act.wait_ge(h_ready, HT * c + m + 1)
                    act.activation(hid[:, m, :], ps[:, 2 + (len(MADE) + m) % 4, :], ACT.Gelu,
                                   bias=b1_col[:, m:m + 1], scale=alpha1[:, m:m + 1]).then_inc(h_taken, 1)

            def chunk(c):
                root(c + 1)
                gelus(c, range(HT // 2))
                take_xt(c + 1)
                gelus(c, range(HT // 2, HT))

            root(0)
            take_xt(0)
            for b in range(TURNS):
                turned_signs(b)
            chunk(0)
            with act.Fori(1, CHUNKS - 1) as c:
                chunk(c)
            gelus(CHUNKS - 1, range(HT))

            def exp(n, kt):
                at_least(act, pv_done, QT * n + kt - 1)
                for c in range(CPB):
                    act.wait_ge(scores_ready, ALL_CHUNKS * n + CPB * kt + c + 1)
                    if c == 0 and kt >= QT - 4:
                        act.wait_ge(scores_biased, 4 * n + kt - (QT - 4) + 1)
                    place = place_of(CPB * (kt - 1) + c)
                    act.activation(exps[:, kt % 2, c * CHUNK:(c + 1) * CHUNK], ps[:, bank_at(place), :],
                                   ACT.Exp).then_inc(exp_done, 1)

            def take_att(n):
                act.wait_ge(pv_done, QT * (n + 1))
                act.activation(att_t[:, :], ps[:, ATT_BANK, :], ACT.Copy).then_inc(att_copied, 1)

            def take_peak(n):
                act.wait_ge(peak_turned, n + 1)
                at_least(act, peak_loaded, 16 * n)
                early = isinstance(n, int) and n == 0
                bank = bank_at(FIRST_PEAK_PLACE if early else PEAK_PLACE)
                act.activation(peak_rows[:, :], ps[:, bank, :].bitcast(BF16)[0:PARTS * QT, 0:P],
                               ACT.Copy).then_inc(peak_copied, 1)

            def head(n, first=False, ahead=True, more=True):
                for kt in range(1, STEPS + 1):
                    if kt == 1 and not first:
                        take_att(n - 1)
                    if kt == PEAK_STEP and ahead:
                        take_peak(n + 1)
                    if kt < STEPS:
                        exp(n, kt)
                    elif more:
                        exp(n + 1, 0)

            take_peak(0)
            exp(0, 0)
            head(0, first=True)
            with act.Fori(1, NHEAD - 1) as n:
                head(n)
            head(NHEAD - 1, ahead=False, more=False)
            take_att(NHEAD - 1)

            act.wait_ge(att_ok, NHEAD)
            def copy_o(g):
                at_least(act, o_turned, KT * g)
                for t in range(TPC):
                    last = act.activation(o_in[:, t, :].rearrange("p (h d) -> p h d", h=HEADS),
                                          vo[:, bass.ds((g // CPB) * HEADS, HEADS),
                                             bass.ds((g % CPB) * TPC + t, 1), :].rearrange("p h o d -> p h (o d)"),
                                          ACT.Copy)
                last.then_inc(o_copied, 1)

            copy_o(0)
            with act.Fori(1, CHUNKS) as g:
                copy_o(g)

        @block.vector
        def _(dve):
            count = [0]

            def link(ins):
                count[0] += 1
                ins.then_inc(setup_step, 1)
                dve.wait_ge(setup_step, count[0])

            def layernorm(c, steps):
                dve.wait_ge(x_loaded, 16 * (c + 1))
                slot = bass.ds(c % X_SLOTS, 1)
                for t in range(TPC):
                    last = dve.bn_stats(stats[:, t, :], x_in[:, slot, t, :].rearrange("p a c -> p (a c)"))
                    last.then_inc(ln_step, 1)
                dve.wait_ge(ln_step, steps + TPC)
                dve.memset(wait_here[:, :], 0.0)
                for t in range(TPC):
                    last = dve.bn_aggr(moments[:, t, :], stats[:, t, :])
                last.then_inc(var_ok, 1)
                dve.wait_ge(std_ok, c + 1)
                dve.reciprocal(rstd[:, :], std[:, :]).then_inc(ln_step, 1)
                dve.wait_ge(ln_step, steps + TPC + 1)
                at_least(dve, xt_turned, KT * c)
                for t in range(TPC):
                    last = dve.tensor_scalar(xn[:, t, :], x_in[:, slot, t, :].rearrange("p a c -> p (a c)"),
                                             moments[:, t, 0:1], rstd[:, t:t + 1], ALU.subtract, ALU.mult)
                last.then_inc(xn_ok, 1)

            LN_STEPS = TPC + 1

            def split_xt(c):
                at_least(dve, h_ready, HT * c)
                for k in range(KT):
                    done = 2 * (KT * c + k)
                    dve.wait_ge(xt_ok, KT * c + k + 1)
                    dve.tensor_copy(xt_high[:, k, :], xt[:, k, :]).then_inc(xt_step, 1)
                    dve.wait_ge(xt_step, done + 1)
                    dve.tensor_tensor(xt_rest[:, k, :], xt[:, k, :], xt_high[:, k, :], ALU.subtract).then_inc(xt_step, 1)
                    dve.wait_ge(xt_step, done + 2)
                    dve.tensor_scalar(xt_low[:, k, :], xt_rest[:, k, :], LOW, None, ALU.mult).then_inc(xt_parts_ok, 1)

            def take_qkv(c):
                for i, (what, j) in enumerate(MADE):
                    dve.wait_ge(qkv_ready, 6 * c + i + 1)
                    src = ps[:, 2 + i % 4, :]
                    if what != "v":
                        at = SPLIT.index(i)
                        s = at % 2
                        at_least(dve, split_ok, ITEMS * c + at - 1)
                        b = (bq_col if what == "q" else bk_col)[:, j:j + 1]
                        if what == "q":
                            dve.tensor_scalar(qk_val[:, s, :], src, b, scale[:, 0:1], ALU.add,
                                              ALU.mult).then_inc(qkv_taken, 1)
                        else:
                            dve.tensor_scalar(qk_val[:, s, :], src, b, None, ALU.add).then_inc(qkv_taken, 1)
                    else:
                        for t in range(2):
                            kt = (c % CPB) * TPC + 2 * j + t
                            last = dve.tensor_tensor(
                                vo[:, bass.ds((c // CPB) * HEADS, HEADS), bass.ds(kt, 1), :].rearrange("p h o d -> p h (o d)"),
                                src[:, t * EMB:(t + 1) * EMB].rearrange("p (h d) -> p h d", h=HEADS),
                                bv_row[:, :].rearrange("p (h d) -> p h d", h=HEADS), ALU.add)
                        last.then_inc(qkv_taken, 1)

            def split_hid(c):
                for m in range(HT):
                    dve.wait_ge(h_taken, HT * c + m + 1)
                    dve.tensor_tensor(hid_rest[:, m, :], hid[:, m, :], high_half(hid[:, m, :]),
                                      ALU.subtract).then_inc(hid_step, 1)
                    if m % 2:
                        dve.wait_ge(hid_step, HT * c + m + 1)
                        for k in (m - 1, m):
                            dve.tensor_tensor(hid_low[:, k, :], hid_rest[:, k, :], high_half(hid_rest[:, k, :]),
                                              ALU.subtract).then_inc(hid_parts_ok, 1)

            def take_y(c):
                at_least(dve, base_stored, 16 * c)
                for j in range(2):
                    dve.wait_ge(y_ready, 2 * c + j + 1)
                    dve.tensor_tensor(base[:, 2 * j:2 * j + 2, :], ps[:, 6 + j, :].rearrange("p (t c) -> p t c", t=2),
                                      alpha2_row[:, None, :].to_broadcast([P, 2, EMB]), ALU.mult).then_inc(y_taken[j], 1)

            dve.memset(all_ones, 1.0)
            dve.memset(delta[:, :], 0.0)
            dve.memset(delta_rev[:, :], 0.0)
            link(dve.memset(eps_col[:, :], EPS))
            layernorm(0, 0)
            dve.wait_ge(w_loaded, 16 * LOADS)
            link(dve.tensor_scalar(scale[:, :], scale[:, :], 0.1, 10.0, ALU.max, ALU.min))
            link(dve.tensor_scalar(scale[:, :], scale[:, :], float(EMB) ** 0.5, None, ALU.mult))
            link(dve.reciprocal(scale[:, :], scale[:, :]))
            link(dve.scalar_tensor_tensor(out=sgn_pos, in0=exps[:, 1], scalar=-1.0, in1=exps[:, 1],
                                          op0=ALU.mult, op1=ALU.max))
            link(dve.tensor_reduce(alpha2[:, :], sgn_pos.rearrange("p (t c) -> p t c", t=KT), AX.X, ALU.add))
            link(dve.tensor_scalar(alpha2[:, :], alpha2[:, :], 1.0 / HIDDEN, None, ALU.mult))
            dve.wait_ge(ident_ok, 2)
            for k in range(KT):
                last = dve.tensor_scalar(diag[:, k], ident[:, :], alpha2[:, k:k + 1], None, ALU.mult)
            last.then_inc(alpha2_turned, 1)
            link(dve.scalar_tensor_tensor(out=sgn_neg, in0=exps[:, 0], scalar=-1.0, in1=exps[:, 0],
                                          op0=ALU.mult, op1=ALU.max))
            link(dve.tensor_reduce(alpha1[:, :], sgn_neg.rearrange("p (t c) -> p t c", t=HT), AX.X, ALU.add))
            link(dve.tensor_scalar(alpha1[:, :], alpha1[:, :], 1.0 / EMB, None, ALU.mult))
            for raw, dst in ((exps[:, 0], sgn_pos), (exps[:, 1], sgn_neg)):
                link(dve.tensor_scalar(dst, raw, 0.0, None, ALU.is_gt))
                link(dve.tensor_scalar(raw, raw, 0.0, None, ALU.is_lt))
                last = dve.tensor_tensor(dst, dst, raw, ALU.subtract)
            last.then_inc(signs_ok, 1)
            dve.wait_ge(table_turned, 1)
            dve.tensor_copy(table_t[:, 0:TABLE], ps[0:HEADS, 7, 0:TABLE]).then_inc(y_taken[1], 1)
            dve.wait_ge(y_taken[1], 1)
            link(dve.tensor_scalar(delta[:, 0:TABLE], table_t[:, 0:TABLE], table_t[:, TABLE - 1:TABLE],
                                   scale[0:HEADS, 0:1], ALU.subtract, ALU.mult))
            dve.tensor_copy(delta_rev[:, 0:REV + 1], delta[:, REV::-1]).then_inc(delta_ok, 1)
            dve.wait_ge(alpha2_turned, 2)
            dve.tensor_copy(alpha2_row[:, :], ps[:, 6, 0:EMB]).then_inc(y_taken[0], 1)
            dve.tensor_tensor(b2_row[:, :], b2_row[:, :], bp_row[:, :], ALU.add).then_inc(consts, 1)

            split_xt(0)
            take_qkv(0)
            layernorm(1, LN_STEPS)
            dve.wait_ge(sign_turned, TURNS)
            split_hid(0)
            split_xt(1)

            def chunk(c):
                take_qkv(c)
                layernorm(c + 1, LN_STEPS * (c + 1))
                take_y(c - 1)
                split_hid(c)
                split_xt(c + 1)

            chunk(1)
            with dve.Fori(2, CHUNKS - 1) as c:
                chunk(c)
            take_qkv(CHUNKS - 1)
            take_y(CHUNKS - 2)
            split_hid(CHUNKS - 1)
            take_y(CHUNKS - 1)
            dve.memset(v_ones[:, :, HDIM:VCOLS], 1.0).then_inc(ones_ok, 1)
            dve.memset(k_stack[SROWS:MROWS, :, :], 1.0).then_inc(ones_ok, 1)

            def units(n, s):
                if s == 0:
                    at_least(dve, peak_ok, n)
                for half in range(HALVES):
                    dve.wait_ge(unit_ready, ALL_UNITS * n + HALVES * s + half + 1)
                    bank = MAX_BANKS[half]
                    if s < 4 and half == 1:
                        dve.tensor_reduce(peaks[:, s, 2:3], ps[:, bank, :], AX.X, ALU.max)
                        if s == 0:
                            dve.wait_ge(bias_max_loaded, 16 * (n + 1))
                            dve.memset(wait_here[:, :], 0.0)
                        top = P * s + CHUNK - 1
                        stop = top - CHUNK
                        rev = bias_max[:, top:(stop if stop >= 0 else None):-1]
                        src = ps[:, bank + 1, :]
                        dve.tensor_tensor_reduce(out=src, in0=src, in1=rev, scale=1.0, scalar=-3.0e38,
                                                 op0=ALU.add, op1=ALU.max,
                                                 accum_out=peaks[:, s, 3:4]).then_inc(unit_done, 1)
                    else:
                        dve.tensor_reduce(peaks[:, s, 2 * half:2 * half + 2], ps[:, bank:bank + 2, :],
                                          AX.X, ALU.max).then_inc(unit_done, 1)

            def take_max(n):
                dve.wait_ge(unit_done, ALL_UNITS * (n + 1))
                at_least(dve, peak_split, n)
                dve.tensor_reduce(peak[:, :], peaks[:, :, :], AX.X, ALU.max).then_inc(peak_ok, 1)

            def bias_scores(n, kt):
                t = kt - (QT - 4)
                if t == 0:
                    dve.wait_ge(bias_exp_loaded, 16 * (n + 1))
                dve.wait_ge(scores_ready, ALL_CHUNKS * n + CPB * kt + 1)
                width = P * (t + 1)
                bank = bank_at(place_of(CPB * (kt - 1)))
                dve.tensor_tensor(ps[:, bank, 0:width], ps[:, bank, 0:width], bias_exp[:, width - 1::-1],
                                  ALU.add).then_inc(scores_biased, 1)

            def normalise(n):
                dve.wait_ge(att_turned, n + 1)
                att = ps[:, bank_at(ATT_PLACE), :].rearrange("p (t c d) -> p t c d", t=TPC, c=CPB)
                dve.reciprocal(rden[:, :, :], att[:, :, :, HDIM]).then_inc(rden_ok, 1)
                dve.wait_ge(rden_ok, n + 1)
                dst = vo[:, bass.ds(n, 1), :, :].rearrange("p n (c t) d -> p t (n c) d", t=TPC)
                for t in range(TPC):
                    last = dve.tensor_tensor(dst[:, t], att[:, t, :, 0:HDIM],
                                             rden[:, t, :, None].to_broadcast([P, CPB, HDIM]), ALU.mult)
                last.then_inc(att_ok, 1)

            def head(n, first=False, ahead2=True, ahead1=True):
                for kt in range(1, STEPS + 1):
                    if QT - 4 <= kt < STEPS:
                        bias_scores(n, kt)
                    if kt == ATT_STEP and not first:
                        normalise(n - 1)
                    if kt <= STEPS - AHEAD:
                        if ahead1:
                            units(n + 1, kt + AHEAD - 1)
                            if kt == STEPS - AHEAD:
                                take_max(n + 1)
                    elif ahead2:
                        units(n + 2, kt - (STEPS - AHEAD) - 1)
            for s in range(STEPS):
                units(0, s)
            take_max(0)
            for s in range(AHEAD):
                units(1, s)
            head(0, first=True)
            with dve.Fori(1, NHEAD - 2) as n:
                head(n)
            head(NHEAD - 2, ahead2=False)
            head(NHEAD - 1, ahead2=False, ahead1=False)
            normalise(NHEAD - 1)

            def sum_out(r):
                for i in range(2):
                    g = 2 * r + i
                    at_least(dve, proj_ready, 2 * g)
                    for k in range(KT):
                        dve.wait_ge(o_turned, KT * g + k + 1)
                        dve.tensor_copy(o_t[:, k, :], ps[:, k, :]).then_inc(ot_ok[k], 1)
                    dve.wait_ge(base_loaded[i], 16 * (r + 1))
                    for j in range(2):
                        dve.wait_ge(proj_ready, 2 * g + j + 1)
                        dst = base_in[:, i, 2 * j:2 * j + 2, :].rearrange("p t c -> p (t c)")
                        last = dve.tensor_tensor(dst, ps[:, 2 + j, :], dst, ALU.add)
                    last.then_inc(out_ok, 1)

            sum_out(0)
            with dve.Fori(1, CHUNKS // 2) as r:
                sum_out(r)

        @block.gpsimd
        def _(pool):
            def convert(out, in_):
                shape = list(in_.shape)
                zero = zeros[:, 0:1] if len(shape) == 2 else zeros[:, None, 0:1]
                return pool.tensor_tensor(out, in_, zero.to_broadcast(shape), ALU.add)

            for m in (ident, ident16):
                pool.memset(m[:, :], 0.0).then_inc(split_step, 1)
            pool.memset(peak_parts[:], 0.0).then_inc(ones_ok, 1)
            pool.memset(zeros[:, :], 0.0).then_inc(split_step, 1)
            pool.wait_ge(split_step, 3)
            for m in (ident, ident16):
                pool.affine_select(out=m[:, :], in_=m[:, :], compare_op=ALU.not_equal, fill=1.0, base=0,
                                   pattern=[[-1, P]], channel_multiplier=1).then_inc(ident_ok, 1)
            pool.wait_ge(consts, 1)

            def add_base(c):
                slot = bass.ds(c % X_SLOTS, 1)
                for j in range(2):
                    pool.wait_ge(y_taken[j], c + 2)
                pool.tensor_tensor(base[:], base[:], x_in[:, slot].rearrange("p a t c -> p (a t) c"),
                                   ALU.add).then_inc(base_step, 1)
                pool.wait_ge(base_step, c + 1)
                pool.tensor_tensor(base[:], base[:], b2_row[:, None, :].to_broadcast([P, TPC, EMB]),
                                   ALU.add).then_inc(base_ok, 1)

            def split_qk(c):
                for i in range(ITEMS):
                    at = ITEMS * c + i
                    s = i % 2
                    done = 3 + 3 * at
                    pool.wait_ge(qkv_taken, 6 * c + SPLIT[i] + 1)
                    at_least(pool, part_stored[s], 16 * (2 * c + i // 2))
                    convert(qk_part[:, s, 0, :], qk_val[:, s, :]).then_inc(split_step, 1)
                    pool.wait_ge(split_step, done + 1)
                    pool.tensor_tensor(qk_rest[:, s, :], qk_val[:, s, :], qk_part[:, s, 0, :],
                                       ALU.subtract).then_inc(split_step, 1)
                    pool.wait_ge(split_step, done + 2)
                    convert(qk_part[:, s, 1, :], qk_rest[:, s, :]).then_inc(split_step, 1)
                    pool.wait_ge(split_step, done + 3)
                    pool.tensor_tensor(qk_part[:, s, 2, :], qk_rest[:, s, :], qk_part[:, s, 1, :],
                                       ALU.subtract).then_inc(split_ok, 1)

            split_qk(0)
            with pool.Fori(1, CHUNKS) as c:
                split_qk(c)
                add_base(c - 1)
            add_base(CHUNKS - 1)

            def copy_v(n, part):
                at_least(pool, pv_done, QT * n - (8 if part == 0 else 0))
                rows = slice(8 * part, 8 * part + 8)
                convert(v_ones[:, rows, 0:HDIM],
                                 vo[:, bass.ds(n, 1), rows, :].rearrange("p n t d -> p (n t) d")).then_inc(v_copied, 1)

            def split_peak(n):
                pool.wait_ge(peak_ok, n + 1)
                at_least(pool, peak_turned, n)
                steps = 4 * n
                pool.tensor_tensor(neg_peak[:, 0, :], zeros[:, :], peak[:, :], ALU.subtract).then_inc(peak_step, 1)
                pool.wait_ge(peak_step, steps + 1)
                convert(peak_parts[:, 0, :], neg_peak[:, 0, :]).then_inc(peak_step, 1)
                pool.wait_ge(peak_step, steps + 2)
                pool.tensor_tensor(neg_peak[:, 1, :], neg_peak[:, 0, :], peak_parts[:, 0, :],
                                   ALU.subtract).then_inc(peak_step, 1)
                pool.wait_ge(peak_step, steps + 3)
                convert(peak_parts[:, 1, :], neg_peak[:, 1, :]).then_inc(peak_step, 1)
                pool.wait_ge(peak_step, steps + 4)
                pool.tensor_tensor(peak_parts[:, 2, :], neg_peak[:, 1, :], peak_parts[:, 1, :],
                                   ALU.subtract).then_inc(peak_split, 1)

            pool.wait_ge(qkv_taken, 6 * CHUNKS)
            copy_v(0, 0)
            copy_v(0, 1)
            split_peak(0)
            with pool.Fori(1, NHEAD) as n:
                copy_v(n, 0)
                split_peak(n)
                copy_v(n, 1)


_INS = ['L0_attn_x', 'L0_attn_Wq', 'L0_attn_bq', 'L0_attn_Wk', 'L0_attn_bk', 'L0_attn_Wv', 'L0_attn_bv', 'L0_attn_Wp',
        'L0_attn_bp', 'L0_attn_bias_table', 'L0_attn_temperature', 'L0_ffn_w1', 'L0_ffn_b1', 'L0_ffn_w2', 'L0_ffn_b2']


def kernel(**inputs):
    import numpy as _np
    import concourse.bacc as _bacc
    from concourse import mybir as _mybir
    from concourse.bass_utils import run_bass_kernel_spmd as _run

    nc = _bacc.Bacc("TRN2", target_bir_lowering=False, num_devices=1)
    arrays, args = {}, []
    for name in _INS:
        a = _np.ascontiguousarray(inputs[name])
        arrays[f"in_{name}_dram"] = a
        args.append(nc.dram_tensor(f"in_{name}_dram", a.shape, _mybir.dt.from_np(a.dtype), kind="ExternalInput").ap())
    args.append(nc.dram_tensor("out_0_dram", (BATCH, TOKENS, EMB), F32, kind="ExternalOutput").ap())
    build(nc, *args)
    r = _run(nc, [arrays], core_ids=[0])
    return r.results[0]["out_0_dram"]
```

```python
from contextlib import ExitStack

import concourse.bass as bass
from concourse import mybir

ALU = mybir.AluOpType
ACT = mybir.ActivationFunctionType
AX = mybir.AxisListType
F32 = mybir.dt.float32
BF16 = mybir.dt.bfloat16
F16 = mybir.dt.float16
I32 = mybir.dt.int32

P = 128
BATCH, TOKENS, EMB = 4, 2048, 256
HEADS = 16
HDIM = EMB // HEADS
HIDDEN = 1024
TABLE = 499
EPS = 1e-5

KT = EMB // P
HT = HIDDEN // P
CHUNK = 512
TPC = CHUNK // P
CHUNKS = BATCH * TOKENS // CHUNK
CPB = TOKENS // CHUNK
NHEAD = BATCH * HEADS
QT = TOKENS // P
PARTS = 3
PAIRS = 6
SROWS = PAIRS * HDIM
MROWS = SROWS + PARTS
SLOTS = 3
STACK_LOADS = 2 * PAIRS
VCOLS = 32
STEPS = QT
HALVES = 2
AHEAD = 4
ORDER = "0m1m2v3"
WWIDE = CHUNK + 3 * P
REV = CHUNK + P - 2
DELTA = 1024
ITEMS = 2 * KT
X_SCALE = 2.0 ** 11
TOP = 2.0 ** 12
EXPONENT, ONE_TWICE = 0x7F800000, 0x7F000000
X_SLOTS = 3
WHOLE = 2
MADE = [("q", 0), ("q", 1), ("v", 0), ("v", 1), ("k", 0), ("k", 1)]
ALL_MADE = len(MADE)
SPLIT = [i for i, (what, _) in enumerate(MADE) if what != "v"]


TURN_BANKS = (0, 1, 2)
ATT_BANK = 3
MAX_BANKS = (4, 6)
FIRST_MAX_BANKS = (4, 2)
EARLY = 7
ALL_CHUNKS = QT * CPB
ALL_UNITS = QT * HALVES
ATT_STEP, PEAK_STEP = 3, STEPS - AHEAD + 2
ATT_AT, PEAK_AT = CPB * (ATT_STEP - 1), CPB * (PEAK_STEP - 1)


def place_of(chunk):
    return chunk + (chunk >= ATT_AT) + (chunk >= PEAK_AT)


ATT_PLACE, PEAK_PLACE, FIRST_PEAK_PLACE = ATT_AT, PEAK_AT + 1, -1 - CPB
CHUNK_AT = {place_of(c): c for c in range(-CPB, ALL_CHUNKS)}


def max_bank(head, half):
    return (FIRST_MAX_BANKS if isinstance(head, int) and head == 0 else MAX_BANKS)[half]


def bank_at(place):
    return TURN_BANKS[place % 3]


def at_least(engine, sem, value):
    if isinstance(value, int) and value <= 0:
        return
    engine.wait_ge(sem, value)


def build(nc, x, wq, bq, wk, bk, wv, bv, wp, bp, table, temperature, w1, b1, w2, b2, out):
    with ExitStack() as ctx:
        def sb(name, shape, dt=F32):
            return ctx.enter_context(nc.sbuf_tensor(name, shape, dt))

        def sem(name):
            return ctx.enter_context(nc.semaphore(name))

        parts_dram = nc.dram_tensor("parts_dram", [2, PARTS, BATCH * EMB, TOKENS], BF16).ap()
        base_dram = nc.dram_tensor("base_dram", [BATCH * TOKENS, EMB], F32).ap()
        delta_dram = nc.dram_tensor("delta_dram", [2, HEADS, DELTA], F32).ap()

        ident = sb("ident", [P, P])
        ident16 = sb("ident16", [P, P], BF16)
        scale = sb("scale", [P, 1])
        wproj = sb("wproj", [P, KT, EMB])
        vo = sb("vo", [P, NHEAD, QT, HDIM])

        w_qkv = sb("w_qkv", [P, 3, KT, EMB])
        w_high = sb("w_high", [P, 3, KT, EMB], F16)
        w_low = sb("w_low", [P, 3, KT, EMB], F16)
        sign1 = sb("sign1", [P, KT, HIDDEN], BF16)
        sign2 = sb("sign2", [P, HT, EMB], BF16)
        alpha1 = sb("alpha1", [P, HT])
        alpha2 = sb("alpha2", [P, KT])
        alpha2_row = sb("alpha2_row", [P, EMB])
        bq_col = sb("bq_col", [P, KT])
        bk_col = sb("bk_col", [P, KT])
        b1_col = sb("b1_col", [P, HT])
        bv_row = sb("bv_row", [P, EMB])
        b2_row = sb("b2_row", [P, EMB])
        x_in = sb("x_in", [P, X_SLOTS, TPC, EMB])
        stats = sb("stats", [P, TPC, 6])
        wait_here = sb("wait_here", [P, 1])
        moments = sb("moments", [P, TPC, 2])
        std = sb("std", [P, TPC])
        rstd = sb("rstd", [P, TPC])
        eps_col = sb("eps_col", [P, 1])
        xn = sb("xn", [P, TPC, EMB])
        xt = sb("xt", [P, KT, CHUNK])
        xt_high = sb("xt_high", [P, 2, KT, CHUNK], F16)
        xt_low = sb("xt_low", [P, 2, KT, CHUNK], F16)
        hid = sb("hid", [P, HT, CHUNK])
        hid_high = sb("hid_high", [P, HT, CHUNK], F16)
        hid_low = sb("hid_low", [P, HT, CHUNK], F16)
        hid_bound = sb("hid_bound", [P, HT])
        hid_scale = sb("hid_scale", [P, HT])
        hid_inverse = sb("hid_inverse", [P, HT])
        w_ends = sb("w_ends", [P, 2])
        w_bound = sb("w_bound", [P, 1])
        w_scale = sb("w_scale", [P, 1])
        w_inverse = sb("w_inverse", [P, 1])
        kv_factor = sb("kv_factor", [P, 1])
        q_factor = sb("q_factor", [P, 1])
        qk_val = sb("qk_val", [P, 2, CHUNK])
        qk_rest = sb("qk_rest", [P, 2, CHUNK])
        qk_part = sb("qk_part", [P, 2, PARTS, CHUNK], BF16)
        base = sb("base", [P, TPC, EMB])

        stack_room = sb("stack_room", [P, 2, SLOTS, TOKENS], BF16)
        q_stack = stack_room[:, 0]
        k_stack = stack_room[:, 1]
        exps = hid[:].rearrange("p (a b) c -> p a (b c)", a=2)
        v_ones = sb("v_ones", [P, QT, VCOLS])
        bias_max = xn[:].rearrange("p t c -> p (t c)")[:, 0:WWIDE]
        bias_exp = xt[:, 0]
        peaks = sb("peaks", [P, QT, CPB])
        peak = sb("peak", [P, QT])
        zeros = sb("zeros", [P, QT])
        neg_peak = sb("neg_peak", [P, 2, QT])
        peak_parts = sb("peak_parts", [P, P // QT, QT], BF16)
        peak_rows = sb("peak_rows", [PARTS * QT, P], BF16)
        att_room = sb("att_room", [P, KT, CHUNK])
        att_t = att_room[:, 0]
        rden = sb("rden", [P, TPC, CPB])

        W_HEADS = KT * HIDDEN // (QT * HDIM)
        w_raw = (exps[:, 0], vo[:, NHEAD - W_HEADS:NHEAD].rearrange("p n t d -> p (n t d)"))
        signs = (k_stack[:, 0], k_stack[:, 1])
        negative = k_stack[:, 2]
        room = q_stack.rearrange("p s t -> p (s t)").bitcast(F32)
        table_in = room[:, 0:4 * HEADS].rearrange("p (t h) -> p t h", t=4)
        bp_row = room[:, EMB:2 * EMB]
        table_t = room[0:HEADS, 2 * EMB:2 * EMB + TABLE]
        delta = room[0:HEADS, DELTA:2 * DELTA]
        delta_rev = room[0:HEADS, 2 * DELTA:3 * DELTA]
        diag = base[:, 0:KT, 0:P]
        w_diag = base[:, KT + 1, 0:P]
        all_ones = base[:, KT, 0:P]
        o_in = (xn, base)
        o_t = (xt, att_room)
        base_in = x_in

        ps = ctx.enter_context(nc.psum_tensor("ps", [P, 8, CHUNK], F32))

        proj_loaded = sem("proj_loaded")
        w1_loaded = sem("w1_loaded")
        w_loaded = sem("w_loaded")
        consts = sem("consts")
        ident_ok = sem("ident_ok")
        setup_step = sem("setup_step")
        signs_ok = sem("signs_ok")
        w_diag_ok = sem("w_diag_ok")
        w_parts_ok = sem("w_parts_ok")
        alpha1_ok = sem("alpha1_ok")
        scales_ok = sem("scales_ok")
        alpha2_turned = sem("alpha2_turned")
        sign_turned = sem("sign_turned")
        sign_copied = sem("sign_copied")
        table_turned = sem("table_turned")
        table_copied = sem("table_copied")
        alpha2_copied = sem("alpha2_copied")
        delta_ok = sem("delta_ok")
        delta_stored = sem("delta_stored")
        x_loaded = sem("x_loaded")
        ln_step = sem("ln_step")
        var_ok = sem("var_ok")
        std_ok = sem("std_ok")
        xn_ok = sem("xn_ok")
        xt_turned = sem("xt_turned")
        xt_ok = sem("xt_ok")
        xt_high_ok = sem("xt_high_ok")
        xt_parts_ok = sem("xt_parts_ok")
        hid_high_ok = sem("hid_high_ok")
        hid_parts_ok = sem("hid_parts_ok")
        qkv_ready = sem("qkv_ready")
        qkv_taken = sem("qkv_taken")
        h_ready = sem("h_ready")
        h_taken = sem("h_taken")
        y_ready = sem("y_ready")
        y_taken = [sem("y_taken0"), sem("y_taken1")]
        blank_ok = sem("blank_ok")
        part1_ok = sem("part1_ok")
        rest_ok = sem("rest_ok")
        part2_ok = sem("part2_ok")
        split_ok = sem("split_ok")
        base_step = sem("base_step")
        base_ok = sem("base_ok")
        base_stored = sem("base_stored")
        part_stored = [sem("part_stored0"), sem("part_stored1")]
        stack_loaded = sem("stack_loaded")
        bias_max_loaded = sem("bias_max_loaded")
        bias_exp_loaded = sem("bias_exp_loaded")
        ones_ok = sem("ones_ok")
        unit_ready = sem("unit_ready")
        unit_done = sem("unit_done")
        peak_ok = sem("peak_ok")
        peak_step = sem("peak_step")
        peak_split = sem("peak_split")
        peak_turned = sem("peak_turned")
        peak_copied = sem("peak_copied")
        peak_loaded = sem("peak_loaded")
        scores_ready = sem("scores_ready")
        scores_biased = sem("scores_biased")
        exp_done = sem("exp_done")
        v_copied = sem("v_copied")
        pv_done = sem("pv_done")
        att_copied = sem("att_copied")
        att_turned = sem("att_turned")
        rden_ok = sem("rden_ok")
        att_ok = sem("att_ok")
        base_loaded = [sem("base_loaded0"), sem("base_loaded1")]
        o_copied = sem("o_copied")
        o_turned = sem("o_turned")
        ot_ok = [sem("ot_ok0"), sem("ot_ok1")]
        proj_ready = sem("proj_ready")
        out_ok = sem("out_ok")
        out_stored = [sem("out_stored0"), sem("out_stored1")]

        x_rows = x.rearrange("b (g t p) c -> p (b g) t c", t=TPC, p=P)
        out_rows = out.rearrange("b (g t p) c -> p (b g) t c", t=TPC, p=P)
        base_rows = base_dram.rearrange("(g t p) c -> p g t c", t=TPC, p=P)

        PROJ_LOADS, W1_LOADS, LOADS = 7, 2, 6
        AHEAD_OF_TURNS = 6
        SIGN_GROUPS = HT * KT // TPC

        block = ctx.enter_context(nc.Block())

        @block.sync
        def _(sp):
            def row(v):
                return bass.AP(tensor=v.tensor, offset=v.offset, ap=[[0, P], [1, v.shape[0]]])

            def weight(w):
                return w.rearrange("(t p) c -> p t c", p=P)

            sp.dma_start(x_in[:, 0], x_rows[:, 0]).then_inc(x_loaded, 16)
            sp.dma_start(w_qkv[:, 0], weight(wq)).then_inc(proj_loaded, 16)
            sp.dma_start(scale[:, :], row(temperature)).then_inc(proj_loaded, 16)
            sp.dma_start(bq_col[:, :], bq.rearrange("(t p) -> p t", p=P),
                         allow_slow_non_contiguous=True).then_inc(proj_loaded, 16)
            sp.dma_start(bk_col[:, :], bk.rearrange("(t p) -> p t", p=P),
                         allow_slow_non_contiguous=True).then_inc(proj_loaded, 16)
            sp.dma_start(bv_row[:, :], row(bv)).then_inc(proj_loaded, 16)
            sp.dma_start(w_qkv[:, 2], weight(wv)).then_inc(proj_loaded, 16)
            sp.dma_start(w_qkv[:, 1], weight(wk)).then_inc(proj_loaded, 16)
            sp.dma_start(b1_col[:, :], b1.rearrange("(t p) -> p t", p=P),
                         allow_slow_non_contiguous=True).then_inc(w1_loaded, 16)
            sp.dma_start(w_raw[0].rearrange("p (t c) -> p t c", t=HT), weight(w1)).then_inc(w1_loaded, 16)
            sp.dma_start(table_in[:, 0:3], table[0:3 * P, :].rearrange("(t p) h -> p t h", p=P)).then_inc(w_loaded, 16)
            sp.dma_start(table_in[0:TABLE - 3 * P, 3], table[3 * P:TABLE, :]).then_inc(w_loaded, 16)
            sp.dma_start(b2_row[:, :], row(b2)).then_inc(w_loaded, 16)
            sp.dma_start(bp_row[:, :], row(bp)).then_inc(w_loaded, 16)
            sp.dma_start(w_raw[1].rearrange("p (t c) -> p t c", t=KT), weight(w2)).then_inc(w_loaded, 16)
            sp.dma_start(wproj[:], weight(wp)).then_inc(w_loaded, 16)

            def load_x(c):
                sp.wait_ge(x_loaded, 16 * c)
                sp.dma_start(x_in[:, bass.ds(c % X_SLOTS, 1)], x_rows[:, bass.ds(c, 1)]).then_inc(x_loaded, 16)

            def store_parts(c):
                rows = (c // CPB) * EMB
                cols = (c % CPB) * CHUNK
                for i in range(ITEMS):
                    sp.wait_ge(split_ok, ITEMS * c + i + 1)
                    dst = parts_dram[i // KT, :, bass.ds(rows + (i % KT) * P, P), bass.ds(cols, CHUNK)]
                    sp.dma_start(dst.rearrange("a r c -> r a c"), qk_part[:, i % 2]).then_inc(part_stored[i % 2], 16)

            def store_base(c):
                sp.wait_ge(base_ok, c + 1)
                sp.dma_start(base_rows[:, bass.ds(c, 1)], base[:]).then_inc(base_stored, 16)

            def load_stack(n):
                slot = n % SLOTS
                at_least(sp, stack_loaded, 16 * STACK_LOADS * n)
                at = 0
                for a in range(PARTS):
                    k = PARTS - a
                    for j in range(k):
                        sp.dma_start(q_stack[at + j * HDIM:at + (j + 1) * HDIM, bass.ds(slot, 1), :],
                                     parts_dram[0, a, bass.ds(n * HDIM, HDIM), :]).then_inc(stack_loaded, 16)
                    for j in range(k):
                        sp.dma_start(k_stack[at + j * HDIM:at + (j + 1) * HDIM, bass.ds(slot, 1), :],
                                     parts_dram[1, j, bass.ds(n * HDIM, HDIM), :]).then_inc(stack_loaded, 16)
                    at += k * HDIM

            def toeplitz(which, n, width):
                r = delta_dram[which, bass.ds(n % HEADS, 1), 0:width]
                return bass.AP(tensor=r.tensor, offset=r.offset, ap=[[1, P], [1, width]])

            def load_bias_max(n):
                if not isinstance(n, int) or n > 0:
                    sp.wait_ge(unit_done, ALL_UNITS * (n - 1) + 4 * HALVES)
                sp.dma_start(bias_max[:, :], toeplitz(0, n, WWIDE)).then_inc(bias_max_loaded, 16)

            load_x(1)
            load_x(2)
            store_parts(0)
            store_parts(1)
            sp.wait_ge(delta_ok, 1)
            sp.dma_start(delta_dram[0], delta).then_inc(delta_stored, 16)
            sp.dma_start(delta_dram[1], delta_rev).then_inc(delta_stored, 16)
            store_base(0)
            load_x(3)
            with sp.Fori(2, CHUNKS - 2) as c:
                store_parts(c)
                store_base(c - 1)
                load_x(c + 2)
            store_parts(CHUNKS - 2)
            store_base(CHUNKS - 3)
            for i in range(2):
                sp.wait_ge(part_stored[i], 16 * 2 * CPB)
            sp.wait_ge(delta_stored, 2 * 16)
            sp.wait_ge(sign_turned, 2 * SIGN_GROUPS)
            sp.wait_ge(xt_turned, KT * CHUNKS)
            load_stack(0)
            load_bias_max(0)
            load_stack(1)
            store_parts(CHUNKS - 1)
            store_base(CHUNKS - 2)
            store_base(CHUNKS - 1)
            for i in range(2):
                sp.wait_ge(part_stored[i], 16 * 2 * CHUNKS)
            sp.wait_ge(base_stored, 16 * CHUNKS)

            def load_bias_exp(n):
                at_least(sp, scores_biased, 4 * n)
                sp.dma_start(bias_exp[:, :], toeplitz(1, n, CHUNK)).then_inc(bias_exp_loaded, 16)

            def load_peak(n):
                sp.wait_ge(peak_copied, n + 1)
                dst = q_stack[SROWS:MROWS, bass.ds(n % SLOTS, 1), :].rearrange("a s (t p) -> a (s t) p", p=P)
                sp.dma_start(dst, peak_rows[:, :]).then_inc(peak_loaded, 16)

            load_bias_max(1)
            load_peak(0)

            def head_loads(n, stack=True, peaks_too=True):
                if stack:
                    at_least(sp, scores_ready, ALL_CHUNKS * n)
                    load_stack(n + 2)
                load_bias_exp(n)
                if stack:
                    load_bias_max(n + 2)
                if peaks_too:
                    load_peak(n + 1)

            head_loads(0)
            with sp.Fori(1, NHEAD - 2) as n:
                head_loads(n)
            head_loads(NHEAD - 2, stack=False)
            head_loads(NHEAD - 1, stack=False, peaks_too=False)

            def load_base(g, j):
                sp.dma_start(base_in[:, j], base_rows[:, bass.ds(g, 1)]).then_inc(base_loaded[j], 16)

            def store_out(g, j):
                sp.wait_ge(out_ok, g + 1)
                sp.dma_start(out_rows[:, bass.ds(g, 1)], base_in[:, j]).then_inc(out_stored[j], 16)

            load_base(0, 0)
            load_base(1, 1)
            with sp.Fori(0, CHUNKS // 2 - 1) as r:
                for j in range(2):
                    store_out(2 * r + j, j)
                    sp.wait_ge(out_stored[j], 16 * (r + 1))
                    load_base(2 * r + j + 2, j)
            for j in range(2):
                store_out(CHUNKS - 2 + j, j)
            for j in range(2):
                sp.wait_ge(out_stored[j], 16 * (CHUNKS // 2))

        @block.tensor
        def _(pe):
            def turn_x(c):
                pe.wait_ge(xn_ok, c + 1)
                for k in range(KT):
                    at_least(pe, xt_ok, KT * c - KT + k + 1)
                    for t in range(TPC):
                        last = pe.transpose(ps[:, k, t * P:(t + 1) * P], xn[:, t, k * P:(k + 1) * P], ident[:, :])
                    last.then_inc(xt_turned, 1)

            def parts_of(c):
                return (xs[:, bass.ds(c % 2, 1)].rearrange("p a k t -> p (a k) t") for xs in (xt_high, xt_low))

            def qkv(c, items=range(ALL_MADE)):
                whole = isinstance(c, int) and c < WHOLE
                if items[0] == 0 and whole:
                    pe.wait_ge(xt_ok, KT * (c + 1))
                elif items[0] == 0:
                    pe.wait_ge(w_parts_ok, 1)
                    pe.wait_ge(xt_parts_ok, KT * (c + 1))
                high, low = parts_of(c)
                for i in items:
                    what, j = MADE[i]
                    if i < 4:
                        at_least(pe, h_taken, HT * c - 4 + (i + 2) % 4 + 1)
                    else:
                        pe.wait_ge(qkv_taken, ALL_MADE * c + i - 3)
                    bank = 2 + i % 4
                    which = "qkv".index(what)
                    if whole:
                        terms = ((w_qkv, xt),)
                    else:
                        terms = ((w_high, high), (w_high, low), (w_low, high))
                    for t in range(1 if what != "v" else 2):
                        todo = [(k, w, xs) for k in range(KT) for w, xs in terms]
                        for at, (k, w, xs) in enumerate(todo):
                            start, stop = at == 0, at == len(todo) - 1
                            if what != "v":
                                last = pe.matmul(ps[:, bank, :], w[:, which, k, j * P:(j + 1) * P], xs[:, k, :],
                                                 start=start, stop=stop)
                            else:
                                tile = 2 * j + t
                                last = pe.matmul(ps[:, bank, t * EMB:(t + 1) * EMB],
                                                 xs[:, k, tile * P:(tile + 1) * P], w[:, which, k, :],
                                                 start=start, stop=stop)
                    last.then_inc(qkv_ready, 1)

            def hidden(c, tiles):
                if tiles[0] == 0:
                    pe.wait_ge(xt_parts_ok, KT * (c + 1))
                high, low = parts_of(c)
                for m in tiles:
                    i = ALL_MADE + m
                    if m < 4:
                        pe.wait_ge(qkv_taken, ALL_MADE * c + i - 3)
                    else:
                        pe.wait_ge(h_taken, HT * c + m - 3)
                    for k in range(KT):
                        cols = slice(m * P, (m + 1) * P)
                        pe.matmul(ps[:, 2 + i % 4, :], sign1[:, k, cols], high[:, k, :],
                                  start=(k == 0), stop=False)
                        last = pe.matmul(ps[:, 2 + i % 4, :], sign1[:, k, cols], low[:, k, :],
                                         start=False, stop=(k == KT - 1))
                    last.then_inc(h_ready, 1)

            def ffn_out(c, between=None):
                for j in range(2):
                    at_least(pe, y_taken[j], c)
                    for t in range(2):
                        tile = 2 * j + t
                        cols = slice(tile * P, (tile + 1) * P)
                        for m in range(HT):
                            if tile == 0:
                                pe.wait_ge(hid_parts_ok, HT * c + m + 1)
                            dst = ps[:, 6 + j, t * EMB:(t + 1) * EMB]
                            pe.matmul(dst, hid_high[:, m, cols], sign2[:, m, :], start=(m == 0), stop=False)
                            last = pe.matmul(dst, hid_low[:, m, cols], sign2[:, m, :], start=False,
                                             stop=(m == HT - 1))
                            if between and m % 2 and (t, m) != (1, HT - 1):
                                between(tile * HT // 2 + m // 2)
                    last.then_inc(y_ready, 1)
                    if between:
                        between((2 * j + 1) * HT // 2 + HT // 2 - 1)

            def turn_signs(which, groups):
                pe.wait_ge(signs_ok, which + 1)
                for g in groups:
                    if g >= 2:
                        pe.wait_ge(sign_copied, SIGN_GROUPS * which + g - 1)
                    for j in range(TPC):
                        k, t = g % KT, (g // KT) * TPC + j
                        at = (t * KT + k if which == 0 else k * HT + t) * P
                        last = pe.transpose(ps[:, g % 2, :].bitcast(BF16)[:, j * P:(j + 1) * P],
                                            signs[which][:, at:at + P], ident16[:, :])
                    last.then_inc(sign_turned, 1)

            pe.wait_ge(ident_ok, 2)
            turn_x(0)
            pe.wait_ge(proj_loaded, 16 * PROJ_LOADS)
            qkv(0, range(2))
            turn_signs(0, range(2))
            qkv(0, range(2, 4))
            turn_signs(0, range(2, SIGN_GROUPS))
            qkv(0, range(4, ALL_MADE))
            pe.wait_ge(sign_copied, SIGN_GROUPS)
            pe.wait_ge(w_loaded, 16 * LOADS)
            for t in range(4):
                rows = P if t < 3 else TABLE - 3 * P
                last = pe.transpose(ps[0:HEADS, 7, t * P:t * P + rows], table_in[0:rows, t, :], ident[0:rows, 0:rows])
            last.then_inc(table_turned, 1)
            hidden(0, range(AHEAD_OF_TURNS))
            turn_x(1)
            hidden(0, range(AHEAD_OF_TURNS, HT))
            pe.wait_ge(xt_ok, 2 * KT)
            turn_signs(1, range(2))
            qkv(1, range(2))
            turn_signs(1, range(2, SIGN_GROUPS))
            qkv(1, range(2, ALL_MADE))
            pe.wait_ge(sign_copied, 2 * SIGN_GROUPS)
            pe.wait_ge(table_copied, 1)
            ffn_out(0)
            pe.wait_ge(alpha2_turned, 1)
            for k in range(KT):
                pe.matmul(ps[:, 0, k * P:(k + 1) * P], all_ones, diag[:, k], start=True, stop=True)
            pe.wait_ge(w_diag_ok, 1)
            pe.matmul(ps[:, 0, EMB:EMB + P], all_ones, w_diag, start=True, stop=True).then_inc(alpha2_turned, 1)
            hidden(1, range(HT // 2))
            pe.wait_ge(alpha2_copied, 1)
            turn_x(2)
            hidden(1, range(HT // 2, HT))

            def chunk(c):
                qkv(c)
                ffn_out(c - 1)
                turn_x(c + 1)
                hidden(c, range(HT))

            with pe.Fori(2, CHUNKS - 1) as c:
                chunk(c)
            qkv(CHUNKS - 1)
            ffn_out(CHUNKS - 2)
            hidden(CHUNKS - 1, range(HT))

            def unit(n, s, half):
                if s == 0 and half == 0:
                    pe.wait_ge(stack_loaded, 16 * STACK_LOADS * (n + 1))
                at_least(pe, unit_done, ALL_UNITS * n + HALVES * s + half - 1)
                for j in range(2):
                    at = (2 * half + j) * CHUNK
                    bank = max_bank(n, half) + j
                    last = pe.matmul(ps[:, bank, :],
                                     q_stack[0:SROWS, bass.ds(n % SLOTS, 1), s * P:(s + 1) * P],
                                     k_stack[0:SROWS, bass.ds(n % SLOTS, 1), at:at + CHUNK], start=True, stop=True)
                last.then_inc(unit_ready, 1)

            def early_unit(i):
                if i == 2:
                    pe.wait_ge(h_taken, HT * CHUNKS)
                if i >= 2:
                    unit(0, (i - 2) // HALVES, (i - 2) % HALVES)

            ffn_out(CHUNKS - 1, early_unit)

            def bank_free(n, place):
                before = place - 3
                first, final = (isinstance(n, int) and n == k for k in (0, NHEAD - 1))
                if before == ATT_PLACE and not first:
                    pe.wait_ge(att_ok, n)
                elif before == PEAK_PLACE and not final:
                    pe.wait_ge(peak_copied, n + 2)
                elif before == FIRST_PEAK_PLACE and first:
                    pe.wait_ge(peak_copied, 1)
                else:
                    if before in (ATT_PLACE, PEAK_PLACE):
                        before -= 3
                    if before >= -CPB:
                        pe.wait_ge(exp_done, ALL_CHUNKS * n + CPB + CHUNK_AT[before] + 1)

            def turn_peak(n, body, place):
                pe.wait_ge(peak_split, n + 1)
                bank_free(body, place)
                pe.transpose(ps[:, bank_at(place), :].bitcast(BF16)[:, 0:P],
                             peak_parts[:].rearrange("p a t -> p (a t)"), ident16[:, :]).then_inc(peak_turned, 1)

            def turn_att(n):
                pe.wait_ge(att_copied, n + 1)
                if isinstance(n, int) and n == NHEAD - 1:
                    pe.wait_ge(exp_done, ALL_CHUNKS * NHEAD)
                    pe.wait_ge(att_ok, n)
                else:
                    bank_free(n + 1, ATT_PLACE)
                for t in range(TPC):
                    last = pe.transpose(ps[:, bank_at(ATT_PLACE), t * P:(t + 1) * P], att_t[:, t * P:(t + 1) * P],
                                        ident[:, :])
                last.then_inc(att_turned, 1)

            def scores(n, kt, c, body, chunk):
                if kt == 0 and c == 0:
                    pe.wait_ge(peak_loaded, 16 * (n + 1))
                bank_free(body, place_of(chunk))
                pe.matmul(ps[:, bank_at(place_of(chunk)), :],
                          k_stack[0:MROWS, bass.ds(n % SLOTS, 1), kt * P:(kt + 1) * P],
                          q_stack[0:MROWS, bass.ds(n % SLOTS, 1), c * CHUNK:(c + 1) * CHUNK],
                          start=True, stop=True).then_inc(scores_ready, 1)

            def times_v(n, kt):
                pe.wait_ge(exp_done, ALL_CHUNKS * n + CPB * (kt + 1))
                if kt % 8 == 0:
                    pe.wait_ge(v_copied, 2 * n + kt // 8 + 1)
                if kt == 0:
                    at_least(pe, att_copied, n)
                for c in range(CPB):
                    last = pe.matmul(ps[c * VCOLS:(c + 1) * VCOLS, ATT_BANK, :], v_ones[:, kt, :],
                                     exps[:, kt % 2, c * CHUNK:(c + 1) * CHUNK], start=(kt == 0), stop=(kt == QT - 1))
                last.then_inc(pv_done, 1)

            def head(n, first=False, ahead2=True, ahead1=True, more=True):
                for kt in range(1, STEPS + 1):
                    if kt == ATT_STEP and not first:
                        turn_att(n - 1)
                    if kt == PEAK_STEP and ahead1:
                        turn_peak(n + 1, n, PEAK_PLACE)
                    half = 0
                    for turn in ORDER:
                        if turn == "m":
                            if kt <= STEPS - AHEAD:
                                if ahead1:
                                    unit(n + 1, kt + AHEAD - 1, half)
                            elif ahead2:
                                unit(n + 2, kt - (STEPS - AHEAD) - 1, half)
                            half += 1
                        elif turn == "v":
                            times_v(n, kt - 1)
                        elif kt < STEPS:
                            scores(n, kt, int(turn), n, CPB * (kt - 1) + int(turn))
                        elif more:
                            scores(n + 1, 0, int(turn), n, CPB * (kt - 1) + int(turn))

            for s in range(EARLY, STEPS):
                for half in range(HALVES):
                    unit(0, s, half)
            for j in range(2):
                pe.wait_ge(y_taken[j], CHUNKS)
            pe.wait_ge(ones_ok, 3)
            for s in range(AHEAD):
                for half in range(HALVES):
                    unit(1, s, half)
                if s == 0:
                    turn_peak(0, 0, FIRST_PEAK_PLACE)
            for c in range(CPB):
                scores(0, 0, c, 0, c - CPB)
            head(0, first=True)
            with pe.Fori(1, NHEAD - 2) as n:
                head(n)
            head(NHEAD - 2, ahead2=False)
            head(NHEAD - 1, ahead2=False, ahead1=False, more=False)
            turn_att(NHEAD - 1)
            pe.wait_ge(att_ok, NHEAD)

            def turn_o(g, i):
                pe.wait_ge(o_copied, g + 1)
                for k in range(KT):
                    at_least(pe, ot_ok[k], g - 1)
                    for t in range(TPC):
                        last = pe.transpose(ps[:, 2 * i + k, t * P:(t + 1) * P], o_in[i][:, t, k * P:(k + 1) * P],
                                            ident[:, :])
                    last.then_inc(o_turned, 1)

            def project(g, i):
                for k in range(KT):
                    pe.wait_ge(ot_ok[k], g + 1)
                at_least(pe, out_ok, g - 1)
                for j in range(2):
                    for t in range(2):
                        for k in range(KT):
                            tile = 2 * j + t
                            last = pe.matmul(ps[:, 4 + 2 * i + j, t * EMB:(t + 1) * EMB],
                                             o_t[i][:, k, tile * P:(tile + 1) * P],
                                             wproj[:, k, :], start=(k == 0), stop=(k == KT - 1))
                    last.then_inc(proj_ready, 1)

            def pair(r, more=True):
                turn_o(2 * r + 1, 1)
                project(2 * r, 0)
                if more:
                    turn_o(2 * r + 2, 0)
                project(2 * r + 1, 1)

            turn_o(0, 0)
            pair(0)
            with pe.Fori(1, CHUNKS // 2 - 1) as r:
                pair(r)
            pair(CHUNKS // 2 - 1, more=False)

        @block.scalar
        def _(act):
            def turned_signs(which, groups=range(SIGN_GROUPS)):
                for g in groups:
                    act.wait_ge(sign_turned, SIGN_GROUPS * which + g + 1)
                    src = ps[:, g % 2, :].bitcast(BF16)[:, 0:CHUNK]
                    k, t = g % KT, (g // KT) * TPC
                    if not which:
                        cols = slice(t * P, (t + TPC) * P)
                        act.activation(sign1[:, k, cols], src, ACT.Copy, scale=1.0 / X_SCALE).then_inc(sign_copied, 1)
                    else:
                        if g == 0:
                            act.wait_ge(scales_ok, 1)
                        for j in range(TPC):
                            block, m = src[:, j * P:(j + 1) * P], t + j
                            last = act.activation(sign2[:, m, k * P:(k + 1) * P], block, ACT.Copy,
                                                  scale=hid_scale[:, m:m + 1])
                        last.then_inc(sign_copied, 1)

            def root(c):
                act.wait_ge(var_ok, c + 1)
                act.activation(std[:, :], moments[:, :, 1], ACT.Sqrt, bias=eps_col[:, 0:1]).then_inc(std_ok, 1)

            def take_xt(c):
                at_least(act, qkv_ready, ALL_MADE * c)
                at_least(act, xt_parts_ok, KT * c)
                for k in range(KT):
                    act.wait_ge(xt_turned, KT * c + k + 1)
                    act.activation(xt[:, k, :], ps[:, k, :], ACT.Copy).then_inc(xt_ok, 1)

            def gelus(c, tiles):
                if tiles[0] == 0:
                    at_least(act, hid_parts_ok, HT * c)
                for m in tiles:
                    act.wait_ge(h_ready, HT * c + m + 1)
                    act.activation(hid[:, m, :], ps[:, 2 + (ALL_MADE + m) % 4, :], ACT.Gelu,
                                   bias=b1_col[:, m:m + 1], scale=alpha1[:, m:m + 1]).then_inc(h_taken, 1)

            def parts_qk(c, items):
                for i in items:
                    s = i % 2
                    act.wait_ge(qkv_taken, ALL_MADE * c + SPLIT[i] + 1)
                    at_least(act, part_stored[s], 16 * (2 * c + i // 2))
                    act.activation(qk_part[:, s, 0, :], qk_val[:, s, :], ACT.Copy).then_inc(part1_ok, 1)
                for i in items:
                    s = i % 2
                    act.wait_ge(rest_ok, ITEMS * c + i + 1)
                    act.activation(qk_part[:, s, 1, :], qk_rest[:, s, :], ACT.Copy).then_inc(part2_ok, 1)

            def chunk(c, first=False):
                parts_qk(c, (0, 1))
                root(c + 1)
                parts_qk(c, (2, 3))
                if not first:
                    take_xt(c + 1)
                gelus(c, range(HT // 2))
                if first:
                    take_xt(2)
                gelus(c, range(HT // 2, HT))

            root(0)
            take_xt(0)
            turned_signs(0, range(2))
            parts_qk(0, (0,))
            turned_signs(0, range(2, SIGN_GROUPS))
            parts_qk(0, (1,))
            parts_qk(0, (2,))
            root(1)
            act.wait_ge(alpha1_ok, 1)
            act.wait_ge(w1_loaded, 16 * W1_LOADS)
            gelus(0, range(AHEAD_OF_TURNS - 2))
            parts_qk(0, (3,))
            gelus(0, range(AHEAD_OF_TURNS - 2, AHEAD_OF_TURNS))
            take_xt(1)
            gelus(0, range(AHEAD_OF_TURNS, HT))
            turned_signs(1)
            chunk(1, first=True)
            with act.Fori(2, CHUNKS - 1) as c:
                chunk(c)
            parts_qk(CHUNKS - 1, (0, 1))
            parts_qk(CHUNKS - 1, (2, 3))
            gelus(CHUNKS - 1, range(HT))

            def exp(n, kt):
                at_least(act, pv_done, QT * n + kt - 1)
                for c in range(CPB):
                    act.wait_ge(scores_ready, ALL_CHUNKS * n + CPB * kt + c + 1)
                    if c == 0 and kt >= QT - 4:
                        act.wait_ge(scores_biased, 4 * n + kt - (QT - 4) + 1)
                    place = place_of(CPB * (kt - 1) + c)
                    act.activation(exps[:, kt % 2, c * CHUNK:(c + 1) * CHUNK], ps[:, bank_at(place), :],
                                   ACT.Exp).then_inc(exp_done, 1)

            def take_att(n):
                act.wait_ge(pv_done, QT * (n + 1))
                act.activation(att_t[:, :], ps[:, ATT_BANK, :], ACT.Copy).then_inc(att_copied, 1)

            def take_peak(n):
                act.wait_ge(peak_turned, n + 1)
                at_least(act, peak_loaded, 16 * n)
                early = isinstance(n, int) and n == 0
                bank = bank_at(FIRST_PEAK_PLACE if early else PEAK_PLACE)
                act.activation(peak_rows[:, :], ps[:, bank, :].bitcast(BF16)[0:PARTS * QT, 0:P],
                               ACT.Copy).then_inc(peak_copied, 1)

            def head(n, first=False, ahead=True, more=True):
                for kt in range(1, STEPS + 1):
                    if kt == 1 and not first:
                        take_att(n - 1)
                    if kt == PEAK_STEP and ahead:
                        take_peak(n + 1)
                    if kt < STEPS:
                        exp(n, kt)
                    elif more:
                        exp(n + 1, 0)

            take_peak(0)
            exp(0, 0)
            head(0, first=True)
            with act.Fori(1, NHEAD - 1) as n:
                head(n)
            head(NHEAD - 1, ahead=False, more=False)
            take_att(NHEAD - 1)

            act.wait_ge(att_ok, NHEAD)
            def copy_o(g, i):
                at_least(act, o_turned, KT * (g - 1))
                for t in range(TPC):
                    last = act.activation(o_in[i][:, t, :].rearrange("p (h d) -> p h d", h=HEADS),
                                          vo[:, bass.ds((g // CPB) * HEADS, HEADS),
                                             bass.ds((g % CPB) * TPC + t, 1), :].rearrange("p h o d -> p h (o d)"),
                                          ACT.Copy)
                last.then_inc(o_copied, 1)

            for i in range(2):
                copy_o(i, i)
            with act.Fori(1, CHUNKS // 2) as r:
                for i in range(2):
                    copy_o(2 * r + i, i)

        @block.vector
        def _(dve):
            count = [0]

            def link(ins):
                count[0] += 1
                ins.then_inc(setup_step, 1)
                dve.wait_ge(setup_step, count[0])

            LN_STEPS = TPC + 1

            def moments_of(c):
                steps = LN_STEPS * c
                dve.wait_ge(x_loaded, 16 * (c + 1))
                slot = bass.ds(c % X_SLOTS, 1)
                for t in range(TPC):
                    last = dve.bn_stats(stats[:, t, :], x_in[:, slot, t, :].rearrange("p a c -> p (a c)"))
                    last.then_inc(ln_step, 1)
                dve.wait_ge(ln_step, steps + TPC)
                dve.memset(wait_here[:, :], 0.0)
                for t in range(TPC):
                    last = dve.bn_aggr(moments[:, t, :], stats[:, t, :])
                last.then_inc(var_ok, 1)

            def layernorm(c):
                steps = LN_STEPS * c
                slot = bass.ds(c % X_SLOTS, 1)
                dve.wait_ge(std_ok, c + 1)
                dve.reciprocal(rstd[:, :], std[:, :]).then_inc(ln_step, 1)
                dve.wait_ge(ln_step, steps + TPC + 1)
                at_least(dve, xt_turned, KT * c)
                for t in range(TPC):
                    last = dve.tensor_scalar(xn[:, t, :], x_in[:, slot, t, :].rearrange("p a c -> p (a c)"),
                                             moments[:, t, 0:1], rstd[:, t:t + 1], ALU.subtract, ALU.mult)
                last.then_inc(xn_ok, 1)

            def split_xt(c):
                at_least(dve, h_ready, HT * (c - 1))
                high, low = (xs[:, bass.ds(c % 2, 1)].rearrange("p a k t -> p (a k) t") for xs in (xt_high, xt_low))
                for k in range(KT):
                    dve.wait_ge(xt_ok, KT * c + k + 1)
                    dve.tensor_scalar(high[:, k, :], xt[:, k, :], X_SCALE, None, ALU.mult).then_inc(xt_high_ok, 1)
                for k in range(KT):
                    dve.wait_ge(xt_high_ok, KT * c + k + 1)
                    dve.scalar_tensor_tensor(out=low[:, k, :], in0=xt[:, k, :], scalar=X_SCALE,
                                             in1=high[:, k, :], op0=ALU.mult,
                                             op1=ALU.subtract).then_inc(xt_parts_ok, 1)

            def take_qkv(c, items):
                whole = isinstance(c, int) and c < WHOLE
                for i in items:
                    what, j = MADE[i]
                    dve.wait_ge(qkv_ready, ALL_MADE * c + i + 1)
                    src = ps[:, 2 + i % 4, :]
                    if what != "v":
                        at = SPLIT.index(i)
                        s = at % 2
                        at_least(dve, split_ok, ITEMS * c + at - 1)
                        bias = (bq_col if what == "q" else bk_col)[:, j:j + 1]
                        if whole:
                            factor = scale if what == "q" else None
                        else:
                            factor = q_factor if what == "q" else kv_factor
                        if factor is None:
                            dve.tensor_scalar(qk_val[:, s, :], src, bias, None, ALU.add).then_inc(qkv_taken, 1)
                        else:
                            dve.tensor_scalar(qk_val[:, s, :], src, factor[:, 0:1], bias, ALU.mult,
                                              ALU.add).then_inc(qkv_taken, 1)
                    else:
                        for t in range(2):
                            kt = (c % CPB) * TPC + 2 * j + t
                            dst = vo[:, bass.ds((c // CPB) * HEADS, HEADS), bass.ds(kt, 1), :].rearrange(
                                "p h o d -> p h (o d)")
                            made = src[:, t * EMB:(t + 1) * EMB].rearrange("p (h d) -> p h d", h=HEADS)
                            bias = bv_row[:, :].rearrange("p (h d) -> p h d", h=HEADS)
                            if whole:
                                last = dve.tensor_tensor(dst, made, bias, ALU.add)
                            else:
                                last = dve.scalar_tensor_tensor(out=dst, in0=made, scalar=kv_factor[:, 0:1], in1=bias,
                                                                op0=ALU.mult, op1=ALU.add)
                        last.then_inc(qkv_taken, 1)

            def split_hid(c, tiles=range(HT)):
                for m in tiles[::2]:
                    pair = (m, m + 1)
                    for k in pair:
                        dve.wait_ge(h_taken, HT * c + k + 1)
                        dve.tensor_scalar(hid_high[:, k, :], hid[:, k, :], hid_inverse[:, k:k + 1], None,
                                          ALU.mult).then_inc(hid_high_ok, 1)
                    for k in pair:
                        dve.wait_ge(hid_high_ok, HT * c + k + 1)
                        dve.scalar_tensor_tensor(out=hid_low[:, k, :], in0=hid[:, k, :],
                                                 scalar=hid_inverse[:, k:k + 1], in1=hid_high[:, k, :],
                                                 op0=ALU.mult, op1=ALU.subtract).then_inc(hid_parts_ok, 1)

            def take_y(c, which=range(2)):
                at_least(dve, base_stored, 16 * c)
                for j in which:
                    dve.wait_ge(y_ready, 2 * c + j + 1)
                    dve.tensor_tensor(base[:, 2 * j:2 * j + 2, :], ps[:, 6 + j, :].rearrange("p (t c) -> p t c", t=2),
                                      alpha2_row[:, None, :].to_broadcast([P, 2, EMB]),
                                      ALU.mult).then_inc(y_taken[j], 1)

            def sign(which):
                raw = w_raw[which]
                link(dve.tensor_scalar(negative, raw, 0.0, None, ALU.is_lt))
                dve.scalar_tensor_tensor(out=signs[which], in0=raw, scalar=0.0, in1=negative,
                                         op0=ALU.is_gt, op1=ALU.subtract).then_inc(signs_ok, 1)

            def mean(which, dst, tiles, length):
                raw = w_raw[which]
                dve.wait_ge(signs_ok, which + 1)
                link(dve.scalar_tensor_tensor(out=raw, in0=raw, scalar=-1.0, in1=raw, op0=ALU.mult, op1=ALU.max))
                link(dve.tensor_reduce(dst, raw.rearrange("p (t c) -> p t c", t=tiles), AX.X, ALU.add))
                return dve.tensor_scalar(dst, dst, 1.0 / length, None, ALU.mult)

            def hidden_scales():
                link(dve.scalar_tensor_tensor(out=hid_bound[:, :], in0=b1_col[:, :], scalar=-1.0, in1=b1_col[:, :],
                                              op0=ALU.mult, op1=ALU.max))
                link(dve.scalar_tensor_tensor(out=hid_bound[:, :], in0=alpha1[:, :], scalar=float(EMB),
                                              in1=hid_bound[:, :], op0=ALU.mult, op1=ALU.add))
                powers(hid_bound, hid_scale, hid_inverse).then_inc(scales_ok, 1)

            def powers(bound, scale, inverse):
                link(dve.tensor_scalar(bound[:, :], bound[:, :], 2.0 ** -100, None, ALU.max))
                link(dve.tensor_scalar(scale[:, :].bitcast(I32), bound[:, :].bitcast(I32), EXPONENT, None,
                                       ALU.bitwise_and))
                link(dve.tensor_scalar(inverse[:, :].bitcast(I32), scale[:, :].bitcast(I32), -1, ONE_TWICE,
                                       ALU.mult, ALU.add))
                dve.tensor_scalar(scale[:, :], scale[:, :], 1.0 / TOP, None, ALU.mult)
                return dve.tensor_scalar(inverse[:, :], inverse[:, :], TOP, None, ALU.mult)

            def largest_w():
                flat = w_qkv[:].rearrange("p a t c -> p (a t c)")
                dve.tensor_reduce(w_ends[:, 0:1], flat, AX.X, ALU.max)
                link(dve.tensor_reduce(w_ends[:, 1:2], flat, AX.X, ALU.min))
                link(dve.scalar_tensor_tensor(out=w_bound[:, :], in0=w_ends[:, 1:2], scalar=-1.0, in1=w_ends[:, 0:1],
                                              op0=ALU.mult, op1=ALU.max))
                dve.tensor_scalar(w_diag, ident[:, :], w_bound[:, 0:1], None, ALU.mult).then_inc(w_diag_ok, 1)

            def split_w():
                link(powers(w_bound, w_scale, w_inverse))
                link(dve.tensor_scalar(kv_factor[:, :], w_scale[:, :], 1.0 / X_SCALE, None, ALU.mult))
                dve.tensor_tensor(q_factor[:, :], kv_factor[:, :], scale[:, :], ALU.mult)
                whole, high, low = (w[:].rearrange("p a t c -> p (a t c)") for w in (w_qkv, w_high, w_low))
                link(dve.tensor_scalar(high, whole, w_inverse[:, 0:1], None, ALU.mult))
                dve.scalar_tensor_tensor(out=low, in0=whole, scalar=w_inverse[:, 0:1], in1=high,
                                         op0=ALU.mult, op1=ALU.subtract).then_inc(w_parts_ok, 1)

            dve.memset(all_ones, 1.0)
            dve.memset(delta[:, :], 0.0)
            dve.memset(delta_rev[:, :], 0.0)
            link(dve.memset(eps_col[:, :], EPS))
            moments_of(0)
            layernorm(0)
            dve.wait_ge(proj_loaded, 16 * PROJ_LOADS)
            link(dve.tensor_scalar(scale[:, :], scale[:, :], 0.1, 10.0, ALU.max, ALU.min))
            link(dve.tensor_scalar(scale[:, :], scale[:, :], float(EMB) ** 0.5, None, ALU.mult))
            link(dve.reciprocal(scale[:, :], scale[:, :]))
            link(dve.tensor_scalar(bq_col[:, :], bq_col[:, :], scale[:, 0:1], None, ALU.mult))
            dve.wait_ge(w1_loaded, 16 * W1_LOADS)
            sign(0)
            take_qkv(0, range(2))
            mean(0, alpha1[:, :], HT, EMB).then_inc(alpha1_ok, 1)
            dve.wait_ge(alpha1_ok, 1)
            hidden_scales()
            take_qkv(0, range(2, 4))
            split_xt(0)
            take_qkv(0, range(4, ALL_MADE))
            moments_of(1)
            layernorm(1)
            dve.wait_ge(w_loaded, 16 * LOADS)
            sign(1)
            moments_of(2)
            dve.wait_ge(ident_ok, 2)
            largest_w()
            take_qkv(1, range(2))
            dve.wait_ge(table_turned, 1)
            dve.tensor_copy(table_t[:, 0:TABLE], ps[0:HEADS, 7, 0:TABLE]).then_inc(table_copied, 1)
            dve.tensor_tensor(b2_row[:, :], b2_row[:, :], bp_row[:, :], ALU.add).then_inc(consts, 1)
            split_hid(0, range(HT // 2))
            take_qkv(1, range(2, 4))
            split_hid(0, range(HT // 2, HT))
            take_qkv(1, range(4, ALL_MADE))
            split_xt(1)
            link(mean(1, alpha2[:, :], KT, HIDDEN))
            for k in range(KT):
                last = dve.tensor_scalar(diag[:, k], ident[:, :], alpha2[:, k:k + 1], None, ALU.mult)
            last.then_inc(alpha2_turned, 1)
            layernorm(2)
            dve.wait_ge(table_copied, 1)
            link(dve.tensor_scalar(delta[:, 0:TABLE], table_t[:, 0:TABLE], table_t[:, TABLE - 1:TABLE],
                                   scale[0:HEADS, 0:1], ALU.subtract, ALU.mult))
            dve.tensor_copy(delta_rev[:, 0:REV + 1], delta[:, REV::-1]).then_inc(delta_ok, 1)
            dve.wait_ge(alpha2_turned, 2)
            dve.tensor_copy(alpha2_row[:, :], ps[:, 0, 0:EMB])
            dve.tensor_reduce(w_bound[:, :], ps[:, 0, EMB:EMB + P], AX.X, ALU.max).then_inc(alpha2_copied, 1)
            dve.wait_ge(alpha2_copied, 1)
            split_w()
            take_y(0)
            split_xt(2)
            split_hid(1)

            def chunk(c):
                take_qkv(c, range(2))
                moments_of(c + 1)
                take_qkv(c, range(2, ALL_MADE))
                layernorm(c + 1)
                take_y(c - 1)
                split_xt(c + 1)
                split_hid(c)

            with dve.Fori(2, CHUNKS - 1) as c:
                chunk(c)
            take_qkv(CHUNKS - 1, range(ALL_MADE))
            take_y(CHUNKS - 2)
            dve.memset(v_ones[:, :, HDIM:VCOLS], 1.0).then_inc(ones_ok, 1)
            split_hid(CHUNKS - 1)

            def units(n, s):
                if s == 0:
                    at_least(dve, peak_ok, n)
                for half in range(HALVES):
                    dve.wait_ge(unit_ready, ALL_UNITS * n + HALVES * s + half + 1)
                    bank = max_bank(n, half)
                    if s < 4 and half == 1:
                        dve.tensor_reduce(peaks[:, s, 2:3], ps[:, bank, :], AX.X, ALU.max)
                        if s == 0:
                            dve.wait_ge(bias_max_loaded, 16 * (n + 1))
                            dve.memset(wait_here[:, :], 0.0)
                        top = P * s + CHUNK - 1
                        stop = top - CHUNK
                        rev = bias_max[:, top:(stop if stop >= 0 else None):-1]
                        src = ps[:, bank + 1, :]
                        dve.tensor_tensor_reduce(out=src, in0=src, in1=rev, scale=1.0, scalar=-3.0e38,
                                                 op0=ALU.add, op1=ALU.max,
                                                 accum_out=peaks[:, s, 3:4]).then_inc(unit_done, 1)
                    else:
                        dve.tensor_reduce(peaks[:, s, 2 * half:2 * half + 2], ps[:, bank:bank + 2, :],
                                          AX.X, ALU.max).then_inc(unit_done, 1)

            def take_max(n):
                dve.wait_ge(unit_done, ALL_UNITS * (n + 1))
                at_least(dve, peak_split, n)
                dve.tensor_reduce(peak[:, :], peaks[:, :, :], AX.X, ALU.max).then_inc(peak_ok, 1)

            def bias_scores(n, kt):
                t = kt - (QT - 4)
                if t == 0:
                    dve.wait_ge(bias_exp_loaded, 16 * (n + 1))
                dve.wait_ge(scores_ready, ALL_CHUNKS * n + CPB * kt + 1)
                width = P * (t + 1)
                bank = bank_at(place_of(CPB * (kt - 1)))
                dve.tensor_tensor(ps[:, bank, 0:width], ps[:, bank, 0:width], bias_exp[:, width - 1::-1],
                                  ALU.add).then_inc(scores_biased, 1)

            def normalise(n):
                dve.wait_ge(att_turned, n + 1)
                att = ps[:, bank_at(ATT_PLACE), :].rearrange("p (t c d) -> p t c d", t=TPC, c=CPB)
                dve.reciprocal(rden[:, :, :], att[:, :, :, HDIM]).then_inc(rden_ok, 1)
                dve.wait_ge(rden_ok, n + 1)
                dst = vo[:, bass.ds(n, 1), :, :].rearrange("p n (c t) d -> p t (n c) d", t=TPC)
                for t in range(TPC):
                    last = dve.tensor_tensor(dst[:, t], att[:, t, :, 0:HDIM],
                                             rden[:, t, :, None].to_broadcast([P, CPB, HDIM]), ALU.mult)
                last.then_inc(att_ok, 1)

            def head(n, first=False, ahead2=True, ahead1=True):
                for kt in range(1, STEPS + 1):
                    if QT - 4 <= kt < STEPS:
                        bias_scores(n, kt)
                    if kt == ATT_STEP and not first:
                        normalise(n - 1)
                    if kt <= STEPS - AHEAD:
                        if ahead1:
                            units(n + 1, kt + AHEAD - 1)
                            if kt == STEPS - AHEAD:
                                take_max(n + 1)
                    elif ahead2:
                        units(n + 2, kt - (STEPS - AHEAD) - 1)
            for s in range(EARLY):
                units(0, s)
                if s == 2:
                    take_y(CHUNKS - 1, (0,))
            take_y(CHUNKS - 1, (1,))
            for s in range(EARLY, STEPS):
                units(0, s)
            take_max(0)
            for s in range(AHEAD):
                units(1, s)
            head(0, first=True)
            with dve.Fori(1, NHEAD - 2) as n:
                head(n)
            head(NHEAD - 2, ahead2=False)
            head(NHEAD - 1, ahead2=False, ahead1=False)
            normalise(NHEAD - 1)

            def take_o(g, i):
                at_least(dve, proj_ready, 2 * (g - 1))
                for k in range(KT):
                    dve.wait_ge(o_turned, KT * g + k + 1)
                    dve.tensor_copy(o_t[i][:, k, :], ps[:, 2 * i + k, :]).then_inc(ot_ok[k], 1)

            def sum_out(g, r, i):
                dve.wait_ge(base_loaded[i], 16 * (r + 1))
                for j in range(2):
                    dve.wait_ge(proj_ready, 2 * g + j + 1)
                    dst = base_in[:, i, 2 * j:2 * j + 2, :].rearrange("p t c -> p (t c)")
                    last = dve.tensor_tensor(dst, ps[:, 4 + 2 * i + j, :], dst, ALU.add)
                last.then_inc(out_ok, 1)

            def pair(r, more=True):
                take_o(2 * r + 1, 1)
                sum_out(2 * r, r, 0)
                if more:
                    take_o(2 * r + 2, 0)
                sum_out(2 * r + 1, r, 1)

            take_o(0, 0)
            pair(0)
            with dve.Fori(1, CHUNKS // 2 - 1) as r:
                pair(r)
            pair(CHUNKS // 2 - 1, more=False)

        @block.gpsimd
        def _(pool):
            def convert(out, in_):
                shape = list(in_.shape)
                zero = zeros[:, 0:1] if len(shape) == 2 else zeros[:, None, 0:1]
                return pool.tensor_tensor(out, in_, zero.to_broadcast(shape), ALU.add)

            for m in (ident, ident16):
                pool.memset(m[:, :], 0.0).then_inc(blank_ok, 1)
            pool.memset(peak_parts[:], 0.0).then_inc(ones_ok, 1)
            pool.memset(zeros[:, :], 0.0).then_inc(blank_ok, 1)
            pool.wait_ge(blank_ok, 3)
            for m in (ident, ident16):
                pool.affine_select(out=m[:, :], in_=m[:, :], compare_op=ALU.not_equal, fill=1.0, base=0,
                                   pattern=[[-1, P]], channel_multiplier=1).then_inc(ident_ok, 1)
            def add_base(c):
                slot = bass.ds(c % X_SLOTS, 1)
                for j in range(2):
                    pool.wait_ge(y_taken[j], c + 1)
                pool.tensor_tensor(base[:], base[:], x_in[:, slot].rearrange("p a t c -> p (a t) c"),
                                   ALU.add).then_inc(base_step, 1)
                pool.wait_ge(base_step, c + 1)
                pool.tensor_tensor(base[:], base[:], b2_row[:, None, :].to_broadcast([P, TPC, EMB]),
                                   ALU.add).then_inc(base_ok, 1)

            def rests_qk(c, items):
                for i in items:
                    s = i % 2
                    pool.wait_ge(part1_ok, ITEMS * c + i + 1)
                    pool.tensor_tensor(qk_rest[:, s, :], qk_val[:, s, :], qk_part[:, s, 0, :],
                                       ALU.subtract).then_inc(rest_ok, 1)
                for i in items:
                    s = i % 2
                    pool.wait_ge(part2_ok, ITEMS * c + i + 1)
                    pool.tensor_tensor(qk_part[:, s, 2, :], qk_rest[:, s, :], qk_part[:, s, 1, :],
                                       ALU.subtract).then_inc(split_ok, 1)

            for i in range(ITEMS):
                rests_qk(0, (i,))
            pool.wait_ge(consts, 1)
            with pool.Fori(1, CHUNKS) as c:
                rests_qk(c, (0, 1))
                rests_qk(c, (2, 3))
                add_base(c - 1)
            add_base(CHUNKS - 1)

            def copy_v(n, part):
                at_least(pool, pv_done, QT * n - (8 if part == 0 else 0))
                rows = slice(8 * part, 8 * part + 8)
                convert(v_ones[:, rows, 0:HDIM],
                                 vo[:, bass.ds(n, 1), rows, :].rearrange("p n t d -> p (n t) d")).then_inc(v_copied, 1)

            def split_peak(n):
                pool.wait_ge(peak_ok, n + 1)
                at_least(pool, peak_turned, n)
                steps = 4 * n
                pool.tensor_tensor(neg_peak[:, 0, :], zeros[:, :], peak[:, :], ALU.subtract).then_inc(peak_step, 1)
                pool.wait_ge(peak_step, steps + 1)
                convert(peak_parts[:, 0, :], neg_peak[:, 0, :]).then_inc(peak_step, 1)
                pool.wait_ge(peak_step, steps + 2)
                pool.tensor_tensor(neg_peak[:, 1, :], neg_peak[:, 0, :], peak_parts[:, 0, :],
                                   ALU.subtract).then_inc(peak_step, 1)
                pool.wait_ge(peak_step, steps + 3)
                convert(peak_parts[:, 1, :], neg_peak[:, 1, :]).then_inc(peak_step, 1)
                pool.wait_ge(peak_step, steps + 4)
                pool.tensor_tensor(peak_parts[:, 2, :], neg_peak[:, 1, :], peak_parts[:, 1, :],
                                   ALU.subtract).then_inc(peak_split, 1)

            pool.wait_ge(sign_turned, 2 * SIGN_GROUPS)
            pool.wait_ge(base_ok, CHUNKS)
            pool.memset(k_stack[SROWS:MROWS, :, :], 1.0).then_inc(ones_ok, 1)
            pool.wait_ge(ones_ok, 3)
            pool.wait_ge(qkv_taken, ALL_MADE * CHUNKS)
            copy_v(0, 0)
            copy_v(0, 1)
            split_peak(0)
            with pool.Fori(1, NHEAD) as n:
                copy_v(n, 0)
                split_peak(n)
                copy_v(n, 1)


_INS = ['L0_attn_x', 'L0_attn_Wq', 'L0_attn_bq', 'L0_attn_Wk', 'L0_attn_bk', 'L0_attn_Wv', 'L0_attn_bv', 'L0_attn_Wp',
        'L0_attn_bp', 'L0_attn_bias_table', 'L0_attn_temperature', 'L0_ffn_w1', 'L0_ffn_b1', 'L0_ffn_w2', 'L0_ffn_b2']


def kernel(**inputs):
    import numpy as _np
    import concourse.bacc as _bacc
    from concourse import mybir as _mybir
    from concourse.bass_utils import run_bass_kernel_spmd as _run

    nc = _bacc.Bacc("TRN2", target_bir_lowering=False, num_devices=1)
    arrays, args = {}, []
    for name in _INS:
        a = _np.ascontiguousarray(inputs[name])
        arrays[f"in_{name}_dram"] = a
        args.append(nc.dram_tensor(f"in_{name}_dram", a.shape, _mybir.dt.from_np(a.dtype), kind="ExternalInput").ap())
    args.append(nc.dram_tensor("out_0_dram", (BATCH, TOKENS, EMB), F32, kind="ExternalOutput").ap())
    build(nc, *args)
    r = _run(nc, [arrays], core_ids=[0])
    return r.results[0]["out_0_dram"]
```
